# Optimizing a Trainium2 kernel written in Bass

```python
import numpy as np
import jax
import jax.numpy as jnp

def _softmax(x, axis=-1):
    return jax.nn.softmax(x, axis=axis)

def _gelu(x):
    return jax.nn.gelu(x, approximate=True)

def _silu(x):
    return jax.nn.silu(x)

def _sigmoid(x):
    return jax.nn.sigmoid(x)

def _layernorm(x, axis=-1, eps=1e-05):
    m = jnp.mean(x, axis=axis, keepdims=True)
    v = jnp.var(x, axis=axis, keepdims=True)
    return (x - m) / jnp.sqrt(v + eps)

def _scatter_add(tgt, idx, src, axis=0):
    return tgt.at[idx].add(src)

def _segment_sum(src, seg, n):
    return jax.ops.segment_sum(src, seg, n)
kernel_name = 'mk_flamingo_gated_d1_seqx_r4_19befd'

def setup_inputs(seed: int=0):
    np.random.seed(seed)
    _w = jnp.asarray

    def _rec_inputs():
        import jax
        import jax.numpy as jnp
        _rk = jax.random.key(seed)
        x = -0.0003929 + 0.9999 * jax.random.normal(jax.random.fold_in(_rk, 1), (8, 112, 256), jnp.float32)
        _lenS = 112 - jax.random.randint(jax.random.fold_in(_rk, 7), (8,), 0, max(1, 112 // 4) + 1, jnp.int32)
        _lenS2 = 375 - jax.random.randint(jax.random.fold_in(_rk, 8), (8,), 0, max(1, 375 // 4) + 1, jnp.int32)
        _ctx_768P = jax.random.normal(jax.random.fold_in(_rk, 11), (8, 16, 192), jnp.float32)
        _ctx_768c = jax.random.dirichlet(jax.random.fold_in(_rk, 511), 0.3 * jnp.ones((16,), jnp.float32), (8, 375))
        _ctx_768t = jnp.einsum('bsk,bkd->bsd', _ctx_768c, _ctx_768P)
        _ctx_768t = _ctx_768t * jax.lax.rsqrt(jnp.mean(jnp.square(_ctx_768t)) + 1e-12) * 0.953939
        ctx_768 = 2.09791e-05 + 1.00001 * (_ctx_768t + 0.3 * jax.random.normal(jax.random.fold_in(_rk, 611), (8, 375, 192), jnp.float32))
        _g = jax.random.normal(jax.random.fold_in(_rk, 9001), (2, 1), jnp.float32)
        _g = jnp.sign(_g) * jnp.maximum(jnp.abs(_g), 1.0) + (_g == 0) * 1.0
        g_xattn = _g[0]
        g_ffn = _g[1]
        return (x, ctx_768, g_xattn, g_ffn)
    x, ctx_768, g_xattn, g_ffn = _rec_inputs()

    def _L0_xattn_setup():
        import jax, jax.numpy as jnp
        import numpy as np
        QUERY_DIM = 256
        KEY_DIM = 192
        NUM_HEADS = 16
        HEAD_DIM = QUERY_DIM // NUM_HEADS
        SCALE = HEAD_DIM ** (-0.5)
        key = jax.random.key(seed)
        ks = jax.random.split(key, 11)
        B, Nq, Nk = (4, 1024, 256)
        s_q = QUERY_DIM ** (-0.5)
        s_k = KEY_DIM ** (-0.5)
        return {'query': jax.random.normal(ks[0], (B, Nq, QUERY_DIM), jnp.float32), 'key': jax.random.normal(ks[1], (B, Nk, KEY_DIM), jnp.float32), 'value': jax.random.normal(ks[2], (B, Nk, KEY_DIM), jnp.float32), 'Wq': jax.random.normal(ks[3], (QUERY_DIM, QUERY_DIM), jnp.float32) * s_q, 'bq': jnp.zeros((QUERY_DIM,), jnp.float32), 'Wk': jax.random.normal(ks[4], (KEY_DIM, QUERY_DIM), jnp.float32) * s_k, 'bk': jnp.zeros((QUERY_DIM,), jnp.float32), 'Wv': jax.random.normal(ks[5], (KEY_DIM, QUERY_DIM), jnp.float32) * s_k, 'bv': jnp.zeros((QUERY_DIM,), jnp.float32), 'Wo': jax.random.normal(ks[6], (QUERY_DIM, QUERY_DIM), jnp.float32) * s_q, 'bo': jnp.zeros((QUERY_DIM,), jnp.float32)}
    _L0_xattn_all = _L0_xattn_setup()
    _L0_xattn_in = {k: v for k, v in _L0_xattn_all.items() if k in ('Wq', 'bq', 'Wk', 'bk', 'Wv', 'bv', 'Wo', 'bo')}
    del _L0_xattn_all

    def _L0_ffn_setup():
        import jax, jax.numpy as jnp
        import numpy as np
        H = 256
        E = 8
        B, S = (4, 512)
        key = jax.random.key(seed)
        k1, k2, k3, k4 = jax.random.split(key, 4)
        x = jax.random.normal(k1, (B, S, H), dtype=jnp.float32)
        wg = jax.random.normal(k2, (H, E), dtype=jnp.float32) * 0.02
        W = jax.random.normal(k3, (E, H, H), dtype=jnp.float32) * 0.02
        b = jax.random.normal(k4, (E, H), dtype=jnp.float32) * 0.02
        return {'x': x, 'wg': wg, 'W': W, 'b': b}
    _L0_ffn_all = _L0_ffn_setup()
    _L0_ffn_in = {k: v for k, v in _L0_ffn_all.items() if k in ('wg', 'W', 'b')}
    del _L0_ffn_all
    return {'x': x, 'ctx_768': ctx_768, 'g_xattn': g_xattn, 'g_ffn': g_ffn, 'L0_xattn_Wq': _L0_xattn_in['Wq'], 'L0_xattn_bq': _L0_xattn_in['bq'], 'L0_xattn_Wk': _L0_xattn_in['Wk'], 'L0_xattn_bk': _L0_xattn_in['bk'], 'L0_xattn_Wv': _L0_xattn_in['Wv'], 'L0_xattn_bv': _L0_xattn_in['bv'], 'L0_xattn_Wo': _L0_xattn_in['Wo'], 'L0_xattn_bo': _L0_xattn_in['bo'], 'L0_ffn_wg': _L0_ffn_in['wg'], 'L0_ffn_W': _L0_ffn_in['W'], 'L0_ffn_b': _L0_ffn_in['b']}

def reference(x, ctx_768, g_xattn, g_ffn, L0_xattn_Wq, L0_xattn_bq, L0_xattn_Wk, L0_xattn_bk, L0_xattn_Wv, L0_xattn_bv, L0_xattn_Wo, L0_xattn_bo, L0_ffn_wg, L0_ffn_W, L0_ffn_b):
    import jax
    import jax.numpy as jnp

    def _L0_xattn_ref(query, key, value, Wq, bq, Wk, bk, Wv, bv, Wo, bo):
        import jax, jax.numpy as jnp
        import numpy as np
        QUERY_DIM = 256
        KEY_DIM = 192
        NUM_HEADS = 16
        HEAD_DIM = QUERY_DIM // NUM_HEADS
        SCALE = HEAD_DIM ** (-0.5)
        B, Nq, _ = query.shape
        Nk = key.shape[1]
        q = (query @ Wq + bq).reshape(B, Nq, NUM_HEADS, HEAD_DIM).transpose(0, 2, 1, 3)
        k = (key @ Wk + bk).reshape(B, Nk, NUM_HEADS, HEAD_DIM).transpose(0, 2, 1, 3)
        v = (value @ Wv + bv).reshape(B, Nk, NUM_HEADS, HEAD_DIM).transpose(0, 2, 1, 3)
        attn = jnp.einsum('bhqd,bhkd->bhqk', q, k) * SCALE
        attn = jax.nn.softmax(attn, axis=-1)
        out = jnp.einsum('bhqk,bhkd->bhqd', attn, v)
        out = out.transpose(0, 2, 1, 3).reshape(B, Nq, QUERY_DIM)
        return out @ Wo + bo

    def _L0_ffn_ref(x, wg, W, b):
        import jax, jax.numpy as jnp
        import numpy as np
        H = 256
        E = 8
        B, S = (4, 512)
        Bb, Ss, Hh = x.shape
        Ee = wg.shape[1]
        T = Bb * Ss
        C = T // Ee
        xt = x.reshape(T, Hh)
        logits = xt @ wg
        probs = jax.nn.softmax(logits, axis=-1)
        idx = jnp.argmax(probs, axis=-1)
        mask = jax.nn.one_hot(idx, Ee, dtype=xt.dtype)
        locations = jnp.cumsum(mask, axis=0) - mask
        mask = mask * (locations < C).astype(xt.dtype)
        gate = jnp.sum(probs * mask, axis=-1)
        loc_s = jnp.sum(locations * mask, axis=-1).astype(jnp.int32)
        loc_oh = jax.nn.one_hot(loc_s, C, dtype=xt.dtype)
        dispatch = mask[:, :, None] * loc_oh[:, None, :]
        combine = gate[:, None, None] * dispatch
        exp_in = jnp.einsum('tec,th->ech', dispatch, xt)
        exp_out = jnp.einsum('ech,efh->ecf', exp_in, W) + b[:, None, :]
        out = jnp.einsum('tec,ecf->tf', combine, exp_out)
        return out.reshape(Bb, Ss, Hh)
    x = x + jnp.tanh(g_xattn[0]) * _L0_xattn_ref(_layernorm(x, axis=-1), ctx_768, ctx_768, L0_xattn_Wq, L0_xattn_bq, L0_xattn_Wk, L0_xattn_bk, L0_xattn_Wv, L0_xattn_bv, L0_xattn_Wo, L0_xattn_bo)
    x = x + jnp.tanh(g_ffn[0]) * _L0_ffn_ref(_layernorm(x, axis=-1), L0_ffn_wg, L0_ffn_W, L0_ffn_b)
    return x

_drawn_inputs = setup_inputs


def setup_inputs(seed=0):
    import zlib

    import numpy as np

    out = dict(_drawn_inputs(seed))
    spreads = {'L0_xattn_bq': (0.0, 0.417),
     'L0_xattn_bk': (0.0, 0.8),
     'L0_xattn_bv': (0.0, 0.1),
     'L0_xattn_bo': (0.0, 0.1)}
    factors = {'L0_ffn_b': 8.0}
    for name, (base, spread) in spreads.items():
        noise = np.random.default_rng([zlib.crc32(name.encode()), seed]).standard_normal(out[name].shape)
        drawn = base * np.exp(spread * noise) if base else spread * noise
        out[name] = jnp.asarray(drawn.astype(out[name].dtype))
    for name, factor in factors.items():
        out[name] = (out[name] * factor).astype(out[name].dtype)
    return out
```

```python
from contextlib import ExitStack

import concourse.bass as bass
from concourse import mybir

F32 = mybir.dt.float32
BF16 = mybir.dt.bfloat16
I32 = mybir.dt.int32
ALU = mybir.AluOpType
ACT = mybir.ActivationFunctionType
AX = mybir.AxisListType

B, NQ, D = 8, 112, 256
NK, DC = 375, 192
H, HD = 16, 16
E, CAP = 8, 112
SLOTS = E * CAP
EPS = 1e-5
SCALE = HD ** -0.5
KC = DC // 2
CHUNKS = [(0, 128), (128, 128), (256, NK - 256)]
NCH = len(CHUNKS)
G = H // 4
UNITS = G * NCH
QC = NK
KQ = NK + NQ
K_PART = (0, 0, 0, 1, 1, 2)
Q_PART = (0, 1, 2, 0, 1, 0)
PROD = HD * len(K_PART)
FAR = 4096
RING = 3
AT_XNT, AT_KQ = 2, (4, 6)
AT_STATS, AT_XN, AT_REST = 0, 1, (5, 7)


def heads_of(unit):
    return range(H * unit // UNITS, H * (unit + 1) // UNITS)


def build(nc, x, ctxT, gx, gf, wq, bq, wk, bk, wv, bv, wo, bo, wg, wT, be, out):
    slots_in = nc.dram_tensor("slots_in", (SLOTS, D), F32).ap()
    slots_out = nc.dram_tensor("slots_out", (SLOTS, D), F32).ap()
    with ExitStack() as stack:
        def sb(name, shape, dt=F32):
            return stack.enter_context(nc.sbuf_tensor(name, shape, dt))

        def sem(name):
            return stack.enter_context(nc.semaphore(name))

        wq_sb = sb("wq_sb", [128, 2, D])
        bq_sb = sb("bq_sb", [1, D])
        wk_sb = sb("wk_sb", [KC + 1, 2, D])
        wv_sb = sb("wv_sb", [KC + 1, 2, D])
        wo_sb = sb("wo_sb", [128, G, D])
        wg_sb = sb("wg_sb", [128, 2, E])
        wT_sb = sb("wT_sb", [128, E, 2, D])
        be_sb = sb("be_sb", [NQ, E, D])
        gate_sb = sb("gate_sb", [NQ, 2])
        tanh_sb = sb("tanh_sb", [NQ, 2])
        ident = sb("ident", [128, 128])
        ones_row = sb("ones_row", [1, NQ])
        ones_col = sb("ones_col", [128, 1], BF16)
        half = sb("half", [NQ, 1])
        before = sb("before", [NQ, NQ], BF16)
        every = sb("every", [NQ, NQ], BF16)
        expert_no = sb("expert_no", [NQ, B, E])
        x_sb = sb("x_sb", [NQ, B, D])
        x1_sb = sb("x1_sb", [NQ, B, D])
        xn2_sb = sb("xn2_sb", [NQ, B, D])
        ctx_sb = sb("ctx_sb", [KC + 1, RING, 2, NK])
        st1 = sb("st1", [NQ, 6])
        mv1 = sb("mv1", [NQ, 2])
        ve1 = sb("ve1", [NQ, 1])
        rs1 = sb("rs1", [NQ, 1])
        xn = sb("xn", [NQ, D])
        xnT = sb("xnT", [128, 2, NQ])
        parts = sb("parts", [128, RING, 3, 2, KQ], BF16)
        rest = sb("rest", [128, 2, KQ])
        k6 = sb("k6", [PROD + 3, RING, H, NK], BF16)
        q6 = sb("q6", [PROD + 3, RING, H, NQ], BF16)
        v_sb = sb("v_sb", [128, RING, NCH, H, 32])
        nmax = sb("nmax", [NQ, H])
        mparts = sb("mparts", [H, 3, NQ], BF16)
        mrest = sb("mrest", [H, NQ])
        prob = sb("prob", [128, 2, 4 * NQ])
        den = sb("den", [128, G * NQ])
        rden = sb("rden", [128, G * NQ])
        onorm = sb("onorm", [128, G, NQ])
        st2 = sb("st2", [NQ, 6])
        mv2 = sb("mv2", [NQ, 2])
        ve2 = sb("ve2", [NQ, 1])
        rs2 = sb("rs2", [NQ, 1])
        x2T = sb("x2T", [128, B, 2, NQ])
        lmax = sb("lmax", [NQ, B])
        hit = sb("hit", [NQ, B, E])
        cand = sb("cand", [NQ, B, E])
        idx = sb("idx", [NQ, B])
        mask = sb("mask", [NQ, B, E])
        maskb = sb("maskb", [NQ, B, E], BF16)
        shifted = sb("shifted", [NQ, B, E])
        expd = sb("expd", [NQ, B, E])
        esum = sb("esum", [NQ, B])
        gate = sb("gate", [NQ, B])
        own = sb("own", [NQ, B, E])
        place = sb("place", [NQ, B])
        kept = sb("kept", [NQ, B])
        miss = sb("miss", [NQ, B])
        slotf = sb("slotf", [NQ, B])
        slot = sb("slot", [NQ, B], I32)
        slot2 = sb("slot2", [NQ, B])
        xin = sb("xin", [CAP, E, D])
        xinT = sb("xinT", [128, E, 2, CAP])
        yout = sb("yout", [CAP, E, D])
        yt = sb("yt", [NQ, B, D])
        res = xin

        sc = [stack.enter_context(nc.psum_tensor(f"sc{i}", [128, 512], F32)) for i in range(2)]
        stp = [stack.enter_context(nc.psum_tensor(f"stp{i}", [128, 512], F32)) for i in range(2)]
        pj = [stack.enter_context(nc.psum_tensor(f"pj{i}", [128, 512], F32)) for i in range(2)]
        pv = stack.enter_context(nc.psum_tensor("pv", [128, G, NQ + 16], F32))
        misc = stack.enter_context(nc.psum_tensor("misc", [128, 512], F32))

        s_x = sem("x_loaded")
        s_xrest = sem("x_rest_loaded")
        s_gate = sem("gates_loaded")
        s_tanh = sem("tanh_ready")
        s_w = sem("weights_loaded")
        s_wo = sem("wo_loaded")
        s_zeroed = sem("wo_zeroed")
        s_ident = sem("identity_ready")
        s_ones = sem("ones_ready")
        s_cpe = sem("k_ones_ready")
        s_cact = sem("v_ones_ready")
        s_ctx = sem("ctx_loaded")
        s_ctx1 = sem("ctx_ones_ready")
        s_stat = sem("variance_ready")
        s_rstd = sem("rstd_ready")
        s_xn = sem("xn_ready")
        s_xnT = sem("xnT_in_psum")
        s_xnTe = sem("xnT_ready")
        s_kq = sem("kq_in_psum")
        s_hi = sem("kq_hi_ready")
        s_rest = sem("kq_rest_ready")
        s_parts = sem("kq_parts_ready")
        s_first = sem("first_kq_read")
        s_k6 = sem("kq_rows_laid")
        s_v = sem("v_in_psum")
        s_ve = sem("v_ready")
        s_sc = sem("scores_in_psum")
        s_max = sem("max_taken")
        s_mT = sem("maxT_in_psum")
        s_mh = sem("max_hi_ready")
        s_mp = sem("max_parts_ready")
        s_mrow = sem("max_rows_laid")
        s_st = sem("scoresT_in_psum")
        s_p = sem("probs_ready")
        s_pv = sem("pv_in_psum")
        s_on = sem("normalised")
        s_op = sem("wo_product_in_psum")
        s_xn2 = sem("xn2_ready")
        s_wg = sem("wg_loaded")
        s_wT = sem("experts_loaded")
        s_x2T = sem("x2T_in_psum")
        s_x2Te = sem("x2T_ready")
        s_lg = sem("logits_in_psum")
        s_tri = sem("triangle_ready")
        s_eno = sem("expert_numbers_ready")
        s_mask = sem("mask_ready")
        s_shift = sem("shifted_ready")
        s_exp = sem("router_exp_ready")
        s_place = sem("places_in_psum")
        s_slot = sem("slots_ready")
        s_zero = sem("zero_tile_ready")
        s_slotz = sem("slots_in_zeroed")
        s_scat = sem("tokens_scattered")
        s_xin = [sem(f"expert_{e}_loaded") for e in range(E)]
        s_xinT = sem("xinT_in_psum")
        s_xinTe = sem("xinT_ready")
        s_y = sem("y_in_psum")
        s_yread = sem("y_read")
        s_be = sem("expert_biases_loaded")
        s_yout = sem("y_ready")
        s_stored = sem("y_stored")
        s_gath = [sem(f"tile_{b}_gathered") for b in range(B)]
        s_res = sem("result_ready")
        s_out = sem("out_stored")
        s_chain = sem("vector_chain")
        s_pchain = sem("gpsimd_chain")

        def settle(eng, seen):
            eng.drain()
            for s, n in seen.counts():
                eng.sem_inc(s, -n)
            seen.clear()

        class Seen:

            def __init__(self):
                self.n = {}

            def __call__(self, s, more=1):
                name, had = self.n.get(s.name, (s, 0))
                self.n[s.name] = (s, had + more)
                return had + more

            def counts(self):
                return list(self.n.values())

            def clear(self):
                self.n = {}

        def turns(eng, seen, step):
            for t in range(2):
                step(t, t)
            settle(eng, seen)
            with eng.Fori(0, (B - 2) // RING) as i:
                for k in range(RING):
                    step(2 + k, 2 + k + RING * i)
                settle(eng, seen)
            for t in range(B, B + 2):
                step(t, t)
            settle(eng, seen)

        def front(t):
            return t < B

        def maxima(t):
            return 1 <= t <= B

        def attention(t):
            return t >= 2

        block = stack.enter_context(nc.Block())

        @block.sync
        def _(sp):
            seen = Seen()
            ctx_b = ctxT.rearrange("c p b n -> p b c n")
            sp.dma_start(x_sb[:, 0, :], x[0, :, :]).then_inc(s_x, 16)
            sp.wait_ge(s_ctx1, seen(s_ctx1))
            sp.dma_start(ctx_sb[0:KC, 0, :, :], ctx_b[:, 0, :, :]).then_inc(s_ctx, 16)
            sp.dma_start(wk_sb[0:KC, :, :], wk.rearrange("c p n -> p c n")).then_inc(s_w, 16)
            sp.dma_start(wk_sb[KC:KC + 1, 1, :], bk).then_inc(s_w, 16)
            sp.dma_start(wq_sb[:, :, :], wq.rearrange("c p n -> p c n")).then_inc(s_w, 16)
            sp.dma_start(bq_sb[:, :], bq).then_inc(s_w, 16)
            sp.dma_start(wv_sb[0:KC, :, :], wv.rearrange("c p n -> p c n")).then_inc(s_w, 16)
            sp.dma_start(wv_sb[KC:KC + 1, 1, :], bv).then_inc(s_w, 16)
            sp.dma_start(x_sb[:, 1:B, :], x.rearrange("b p d -> p b d")[:, 1:B, :]).then_inc(s_xrest, 16)

            def step(t, tb):
                if front(t):
                    if t > 0:
                        sp.dma_start(ctx_sb[0:KC, t % RING, :, :],
                                     ctx_b[:, bass.ds(tb, 1), :, :]).then_inc(s_ctx, 16)
                    if t == 0:
                        sp.wait_ge(s_zeroed, seen(s_zeroed))
                        wo_v = wo.rearrange("(a g d) n -> g d a n", g=4, d=HD)
                        for g in range(4):
                            sp.dma_start(wo_sb[32 * g:32 * g + HD, :, :], wo_v[g]).then_inc(s_wo, 16)
                        sp.dma_start(wo_sb[HD:HD + 1, 0, :], bo).then_inc(s_wo, 16)
                    sp.wait_ge(s_parts, seen(s_parts))
                    for j in range(len(K_PART)):
                        rows = slice(HD * j, HD * (j + 1))
                        sp.dma_start(k6[rows, t % RING, :, :],
                                     parts[:, t % RING, K_PART[j], :, 0:NK]).then_inc(s_k6, 16)
                        sp.dma_start(q6[rows, t % RING, :, :],
                                     parts[:, t % RING, Q_PART[j], :, QC:KQ]).then_inc(s_k6, 16)
                if maxima(t):
                    sp.wait_ge(s_mp, seen(s_mp))
                    for j in range(3):
                        sp.dma_start(q6[PROD + j:PROD + j + 1, (t - 1) % RING, :, :],
                                     mparts[:, j, :]).then_inc(s_mrow, 16)

            turns(sp, seen, step)

            sp.wait_ge(s_scat, seen(s_scat, 16 * B))
            for e in range(E):
                sp.dma_start(xin[:, e, :], slots_in[e * CAP:(e + 1) * CAP, :]).then_inc(s_xin[e], 16)
            for e in range(E):
                sp.wait_ge(s_yout, seen(s_yout))
                sp.dma_start(slots_out[e * CAP:(e + 1) * CAP, :], yout[:, e, :]).then_inc(s_stored, 16)
            for b in range(B):
                sp.wait_ge(s_res, seen(s_res))
                sp.dma_start(out[b, :, :], res[:, b, :]).then_inc(s_out, 16)
            sp.wait_ge(s_out, seen(s_out, 16 * B))

        @block.tensor
        def _(pe):
            seen = Seen()
            pe.wait_ge(s_ident, seen(s_ident, 2))

            def transpose_xn():
                pe.wait_ge(s_xn, seen(s_xn))
                for c in range(2):
                    mm = pe.transpose(misc[:, c * NQ:(c + 1) * NQ], xn[:, c * 128:(c + 1) * 128],
                                      ident[0:NQ, 0:NQ])
                mm.then_inc(s_xnT, 1)

            def project_kq(t, m):
                cols = slice(m * 128, (m + 1) * 128)
                if m == 0:
                    pe.wait_ge(s_ctx, seen(s_ctx, 16))
                    pe.wait_ge(s_xnTe, seen(s_xnTe))
                    if t == 0:
                        pe.wait_ge(s_w, seen(s_w, 96))
                if t > 0:
                    pe.wait_ge(s_ve, seen(s_ve))
                for c in range(2):
                    rows = KC + c
                    pe.matmul(pj[m][:, 0:NK], wk_sb[0:rows, c, cols],
                              ctx_sb[0:rows, t % RING, c, :], start=(c == 0), stop=(c == 1))
                for c in range(2):
                    pe.matmul(pj[m][:, QC:KQ], wq_sb[:, c, cols], xnT[:, c, :],
                              start=(c == 0), stop=False)
                pe.matmul(pj[m][:, QC:KQ], bq_sb[:, cols], ones_row[:, :],
                          start=False, stop=True).then_inc(s_kq, 1)

            def project_v(t, m):
                for n, (k0, kn) in enumerate(CHUNKS):
                    if n // 2 != m:
                        continue
                    for c in range(2):
                        rows = KC + c
                        mm = pe.matmul(pj[m][0:kn, (n % 2) * D:(n % 2 + 1) * D],
                                       ctx_sb[0:rows, t % RING, c, k0:k0 + kn],
                                       wv_sb[0:rows, c, :], start=(c == 0), stop=(c == 1))
                mm.then_inc(s_v, 1)

            def scores(b3, h):
                pe.wait_ge(s_max, seen(s_max))
                pe.matmul(sc[h % 2][0:NQ, 0:NK], q6[0:PROD, b3, h, :], k6[0:PROD, b3, h, :],
                          start=True, stop=True).then_inc(s_sc, 1)

            def scores_T(b3, n):
                g, c = divmod(n, NCH)
                k0, kn = CHUNKS[c]
                for j in range(4):
                    h = 4 * g + j
                    mm = pe.matmul(stp[n % 2][0:kn, j * NQ:(j + 1) * NQ],
                                   k6[:, b3, h, k0:k0 + kn], q6[:, b3, h, :], start=True, stop=True)
                mm.then_inc(s_st, 1)

            def probs_v(b3, n):
                g, c = divmod(n, NCH)
                kn = CHUNKS[c][1]
                pe.wait_ge(s_p, seen(s_p))
                for j in range(4):
                    mm = pe.matmul(pv[32 * j:32 * j + 32, g, 0:NQ], v_sb[0:kn, b3, c, 4 * g + j, :],
                                   prob[0:kn, n % 2, j * NQ:(j + 1) * NQ],
                                   start=(c == 0), stop=(c == NCH - 1), tile_position=(0, 32 * j))
                if n == UNITS - 1:
                    mm.then_inc(s_pv, 1)

            def step(t, tb):
                if maxima(t):
                    pe.wait_ge(s_k6, seen(s_k6, 16 * 2 * len(K_PART)))
                if attention(t):
                    pe.wait_ge(s_mrow, seen(s_mrow, 48))
                if t == B:
                    pe.wait_ge(s_ve, seen(s_ve, 2))
                for n in range(UNITS):
                    if attention(t):
                        scores_T((t - 2) % RING, n)
                    if maxima(t):
                        for h in heads_of(n):
                            scores((t - 1) % RING, h)
                    if front(t) and n == AT_XNT:
                        transpose_xn()
                    for m in range(2):
                        if front(t) and n == AT_KQ[m]:
                            project_kq(t, m)
                    if attention(t) and n > 0:
                        probs_v((t - 2) % RING, n - 1)
                if attention(t):
                    probs_v((t - 2) % RING, UNITS - 1)
                if maxima(t):
                    pe.wait_ge(s_max, seen(s_max, 0) + 2)
                    pe.transpose(misc[0:H, 2 * NQ:3 * NQ], nmax[:, :], ident[0:NQ, 0:NQ])\
                        .then_inc(s_mT, 1)
                if front(t):
                    if t == 0:
                        pe.wait_ge(s_first, seen(s_first))
                    project_v(t, 0)
                    project_v(t, 1)
                if t == 1:
                    pe.wait_ge(s_wo, seen(s_wo, 80))
                    pe.wait_ge(s_cpe, seen(s_cpe, RING))
                    pe.wait_ge(s_cact, seen(s_cact))
                if attention(t):
                    pe.wait_ge(s_on, seen(s_on))
                    for g in range(G):
                        mm = pe.matmul(misc[0:NQ, 0:D], onorm[:, g, :], wo_sb[:, g, :],
                                       start=(g == 0), stop=(g == G - 1))
                    mm.then_inc(s_op, 1)

            turns(pe, seen, step)

            pe.wait_ge(s_xn2, seen(s_xn2))
            pe.wait_ge(s_wg, seen(s_wg, 16))

            def logits(b):
                pe.wait_ge(s_x2Te, seen(s_x2Te))
                for c in range(2):
                    mm = pe.matmul(stp[0][0:NQ, b * E:(b + 1) * E], x2T[:, b, c, :], wg_sb[:, c, :],
                                   start=(c == 0), stop=(c == 1))
                return mm

            for b in range(B):
                for c in range(2):
                    mm = pe.transpose(sc[b % 2][:, c * NQ:(c + 1) * NQ],
                                      xn2_sb[:, b, c * 128:(c + 1) * 128], ident[0:NQ, 0:NQ])
                mm.then_inc(s_x2T, 1)
                if b:
                    logits(b - 1)
            logits(B - 1).then_inc(s_lg, 1)

            pe.wait_ge(s_mask, seen(s_mask))
            pe.wait_ge(s_tri, seen(s_tri, 2))
            for b in range(B - 1):
                pe.matmul(stp[1][0:NQ, (b + 1) * E:B * E], every[:, :],
                          maskb[:, b:b + 1, :].to_broadcast([NQ, B - 1 - b, E]),
                          start=(b == 0), stop=False, skip_group_check=True)
            mm = pe.matmul(stp[1][0:NQ, 0:B * E], before[:, :], maskb[:, :, :],
                           start=False, stop=True, skip_group_check=True)
            mm.then_inc(s_place, 1)

            def product(e):
                pe.wait_ge(s_xinTe, seen(s_xinTe))
                if e >= 2:
                    pe.wait_ge(s_yread, seen(s_yread))
                for c in range(2):
                    mm = pe.matmul(pj[e % 2][0:CAP, 0:D], xinT[:, e, c, :], wT_sb[:, e, c, :],
                                   start=(c == 0), stop=(c == 1))
                mm.then_inc(s_y, 1)

            pe.wait_ge(s_wT, seen(s_wT, 16))
            for e in range(E):
                pe.wait_ge(s_xin[e], 16)
                for c in range(2):
                    mm = pe.transpose(sc[e % 2][:, c * CAP:(c + 1) * CAP],
                                      xin[:, e, c * 128:(c + 1) * 128], ident[0:CAP, 0:CAP])
                mm.then_inc(s_xinT, 1)
                if e:
                    product(e - 1)
            product(E - 1)

        @block.scalar
        def _(act):
            seen = Seen()
            for n, g in enumerate((gx, gf)):
                act.dma_start(gate_sb[:, n:n + 1], g.partition_broadcast(NQ)).then_inc(s_gate, 16)
            act.dma_start(wg_sb[:, :, :], wg.rearrange("c p e -> p c e")).then_inc(s_wg, 16)
            act.wait_ge(s_gate, seen(s_gate, 32))
            nc.scalar.activation(tanh_sb[:, :], gate_sb[:, :], ACT.Tanh).then_inc(s_tanh, 1)
            act.dma_start(wT_sb[:, :, :, :], wT.rearrange("e c p f -> p e c f")).then_inc(s_wT, 16)
            act.dma_start(be_sb[:, :, :], be.partition_broadcast(NQ)).then_inc(s_be, 16)
            act.wait_ge(s_zero, seen(s_zero))
            act.dma_start(slots_in.rearrange("(e c) d -> c e d", e=E), yt[:, :, :])\
               .then_inc(s_slotz, 16)

            act.wait_ge(s_ones, seen(s_ones))
            for r in range(RING):
                nc.scalar.activation(k6[PROD:PROD + 3, r, :, :].rearrange("p h n -> p (h n)"),
                                     ones_col[PROD:PROD + 3, :].to_broadcast([3, H * NK]),
                                     ACT.Copy).then_inc(s_cpe, 1)

            def step(t, tb):
                for n in range(UNITS):
                    if attention(t):
                        act.wait_ge(s_st, seen(s_st))
                        kn = CHUNKS[n % NCH][1]
                        nc.scalar.activation(prob[0:kn, n % 2, :], stp[n % 2][0:kn, 0:4 * NQ],
                                             ACT.Exp, scale=SCALE).then_inc(s_p, 1)
                    if front(t) and n == AT_XNT:
                        act.wait_ge(s_xnT, seen(s_xnT))
                        nc.scalar.activation(xnT[:, :, :].rearrange("p c n -> p (c n)"), misc[:, 0:2 * NQ],
                                             ACT.Copy)\
                            .then_inc(s_xnTe, 1)
                    for m in range(2):
                        if front(t) and n == AT_KQ[m]:
                            act.wait_ge(s_kq, seen(s_kq))
                            nc.scalar.activation(parts[:, t % RING, 0, m, :], pj[m][:, 0:KQ],
                                                 ACT.Copy).then_inc(s_hi, 1)
                if maxima(t):
                    act.wait_ge(s_mT, seen(s_mT))
                    nc.scalar.activation(mparts[:, 0, :], misc[0:H, 2 * NQ:3 * NQ], ACT.Copy)\
                        .then_inc(s_mh, 1)
                if front(t):
                    act.wait_ge(s_v, seen(s_v))
                    nc.scalar.activation(v_sb[:, t % RING, 0:2, :, 0:HD],
                                         pj[0][:, :].rearrange("p (c h d) -> p c h d", c=2, h=H),
                                         ACT.Copy).then_inc(s_ve, 1)
                    act.wait_ge(s_v, seen(s_v))
                    kn = CHUNKS[2][1]
                    nc.scalar.activation(v_sb[0:kn, t % RING, 2, :, 0:HD],
                                         pj[1][0:kn, 0:D].rearrange("p (h d) -> p h d", h=H),
                                         ACT.Copy).then_inc(s_ve, 1)

            turns(act, seen, step)

            for b in range(B):
                act.wait_ge(s_x2T, seen(s_x2T))
                nc.scalar.activation(x2T[:, b, :, :].rearrange("p c n -> p (c n)"),
                                     sc[b % 2][:, 0:2 * NQ], ACT.Copy).then_inc(s_x2Te, 1)
            act.wait_ge(s_shift, seen(s_shift))
            nc.scalar.activation(expd[:, :, :], shifted[:, :, :], ACT.Exp).then_inc(s_exp, 1)
            for e in range(E):
                act.wait_ge(s_xinT, seen(s_xinT))
                nc.scalar.activation(xinT[:, e, :, :].rearrange("p c n -> p (c n)"),
                                     sc[e % 2][:, 0:2 * CAP], ACT.Copy).then_inc(s_xinTe, 1)

        @block.vector
        def _(dve):
            seen = Seen()

            def link(ins):
                ins.then_inc(s_chain, 1)
                dve.wait_ge(s_chain, seen(s_chain))

            nc.vector.memset(ctx_sb[KC:KC + 1, :, :, :], 1.0).then_inc(s_ctx1, 1)
            nc.vector.memset(ones_row[:, :], 1.0).then_inc(s_ident, 1)
            nc.vector.memset(wo_sb[:, :, :], 0.0).then_inc(s_zeroed, 1)
            nc.vector.memset(ones_col[:, :], 1.0).then_inc(s_ones, 1)
            nc.vector.memset(yt[:, :, :], 0.0).then_inc(s_zero, 1)
            dve.sem_inc(s_max, 2)
            dve.wait_ge(s_x, seen(s_x, 16))
            dve.wait_ge(s_tanh, seen(s_tanh))

            def step(t, tb):
                if t == 1:
                    dve.wait_ge(s_xrest, seen(s_xrest, 16))
                for n in range(UNITS):
                    if maxima(t):
                        for h in heads_of(n):
                            dve.wait_ge(s_sc, seen(s_sc))
                            nc.vector.tensor_reduce(nmax[:, h:h + 1], sc[h % 2][0:NQ, 0:NK], axis=AX.X,
                                                    op=ALU.max, negate=True).then_inc(s_max, 1)
                    if front(t) and n == AT_STATS:
                        link(nc.vector.bn_stats(st1[:, :], x_sb[:, bass.ds(tb, 1), :]))
                        nc.vector.bn_aggr(mv1[:, :], st1[:, :]).then_inc(s_stat, 1)
                    if front(t) and n == AT_XN:
                        dve.wait_ge(s_rstd, seen(s_rstd))
                        nc.vector.tensor_scalar(xn[:, :], x_sb[:, bass.ds(tb, 1), :], mv1[:, 0:1],
                                                rs1[:, :], ALU.subtract, ALU.mult).then_inc(s_xn, 1)
                    for m in range(2):
                        if front(t) and n == AT_REST[m]:
                            dve.wait_ge(s_hi, seen(s_hi))
                            nc.vector.tensor_tensor(rest[:, m, :], pj[m][:, 0:KQ],
                                                    parts[:, t % RING, 0, m, :], ALU.subtract)\
                                .then_inc(s_rest, 1)
                if t == 0:
                    dve.drain().then_inc(s_first, 1)
                if maxima(t):
                    dve.wait_ge(s_mh, seen(s_mh))
                    link(nc.vector.tensor_tensor(mrest[:, :], misc[0:H, 2 * NQ:3 * NQ],
                                                 mparts[:, 0, :], ALU.subtract))
                    link(nc.vector.tensor_copy(mparts[:, 1, :], mrest[:, :]))
                    nc.vector.tensor_tensor(mparts[:, 2, :], mrest[:, :], mparts[:, 1, :],
                                            ALU.subtract).then_inc(s_mp, 1)
                if attention(t):
                    dve.wait_ge(s_pv, seen(s_pv))
                    link(nc.vector.stream_shuffle(den[:, :].rearrange("p (g n) -> p g n", g=G),
                                                  pv[:, :, 0:NQ], [HD] * 32))
                    link(nc.vector.reciprocal(rden[:, :], den[:, :]))
                    nc.vector.tensor_tensor(onorm[:, :, :], pv[:, :, 0:NQ],
                                            rden[:, :].rearrange("p (g n) -> p g n", g=G),
                                            ALU.mult).then_inc(s_on, 1)
                    dve.wait_ge(s_op, seen(s_op))
                    tok = bass.ds(tb - 2, 1)
                    link(nc.vector.scalar_tensor_tensor(x1_sb[:, tok, :], misc[0:NQ, 0:D],
                                                        tanh_sb[:, 0:1], x_sb[:, tok, :],
                                                        ALU.mult, ALU.add))
                    link(nc.vector.bn_stats(st2[:, :], x1_sb[:, tok, :]))
                    nc.vector.bn_aggr(mv2[:, :], st2[:, :]).then_inc(s_stat, 1)
                    dve.wait_ge(s_rstd, seen(s_rstd))
                    link(nc.vector.tensor_scalar(xn2_sb[:, tok, :], x1_sb[:, tok, :], mv2[:, 0:1],
                                                 rs2[:, :], ALU.subtract, ALU.mult))

            turns(dve, seen, step)
            dve.sem_inc(s_xn2, 1)

            lg = stp[0][0:NQ, 0:B * E].rearrange("p (b e) -> p b e", e=E)
            spread = lambda a: a[:, :].unsqueeze(2).to_broadcast([NQ, B, E])
            dve.wait_ge(s_eno, seen(s_eno))
            dve.wait_ge(s_lg, seen(s_lg))
            link(nc.vector.tensor_reduce(lmax[:, :], lg, axis=AX.X, op=ALU.max))
            nc.vector.tensor_tensor(shifted[:, :, :], lg, spread(lmax), ALU.subtract)\
                .then_inc(s_shift, 1)
            link(nc.vector.tensor_tensor(hit[:, :, :], lg, spread(lmax), ALU.is_equal))
            link(nc.vector.scalar_tensor_tensor(cand[:, :, :], hit[:, :, :], -float(E),
                                                expert_no[:, :, :], ALU.mult, ALU.add))
            link(nc.vector.tensor_reduce(idx[:, :], cand[:, :, :], axis=AX.X, op=ALU.min))
            nc.vector.tensor_tensor(maskb[:, :, :], cand[:, :, :], spread(idx), ALU.is_equal)\
                .then_inc(s_mask, 1)
            dve.wait_ge(s_exp, seen(s_exp))
            link(nc.vector.tensor_reduce(esum[:, :], expd[:, :, :], axis=AX.X, op=ALU.add))
            link(nc.vector.reciprocal(gate[:, :], esum[:, :]))
            dve.wait_ge(s_place, seen(s_place))
            link(nc.vector.tensor_tensor(own[:, :, :],
                                         stp[1][0:NQ, 0:B * E].rearrange("p (b e) -> p b e", e=E),
                                         maskb[:, :, :], ALU.mult))
            link(nc.vector.tensor_reduce(place[:, :], own[:, :, :], axis=AX.X, op=ALU.add))
            link(nc.vector.tensor_scalar(kept[:, :], place[:, :], float(CAP), None, ALU.is_lt))
            link(nc.vector.scalar_tensor_tensor(slotf[:, :], idx[:, :], float(CAP), place[:, :],
                                                ALU.mult, ALU.add))
            link(nc.vector.scalar_tensor_tensor(slot2[:, :], kept[:, :], -float(FAR), slotf[:, :],
                                                ALU.mult, ALU.add))
            nc.vector.tensor_scalar(slot[:, :], slot2[:, :], float(FAR + E * CAP), None, ALU.add)\
                .then_inc(s_slot, 1)
            link(nc.vector.scalar_tensor_tensor(gate[:, :], gate[:, :], tanh_sb[:, 1:2], kept[:, :],
                                                ALU.mult, ALU.mult))
            dve.wait_ge(s_be, seen(s_be, 16))
            for e in range(E):
                dve.wait_ge(s_y, seen(s_y))
                nc.vector.tensor_tensor(yout[:, e, :], pj[e % 2][0:CAP, 0:D], be_sb[:, e, :], ALU.add)\
                    .then_inc(s_yout, 1)
                if e < E - 2:
                    dve.drain().then_inc(s_yread, 1)
            for b in range(B):
                dve.wait_ge(s_gath[b], 16)
                nc.vector.scalar_tensor_tensor(res[:, b, :], yt[:, b, :], gate[:, b:b + 1],
                                               x1_sb[:, b, :], ALU.mult, ALU.add).then_inc(s_res, 1)

        @block.gpsimd
        def _(pool):
            seen = Seen()

            def link(ins):
                ins.then_inc(s_pchain, 1)
                pool.wait_ge(s_pchain, seen(s_pchain))

            link(nc.gpsimd.memset(ident[:, :], 0.0))
            nc.gpsimd.affine_select(out=ident[:, :], in_=ident[:, :], compare_op=ALU.not_equal,
                                    fill=1.0, base=0, pattern=[[-1, 128]],
                                    channel_multiplier=1).then_inc(s_ident, 1)
            link(nc.gpsimd.memset(half[:, :], -0.5))

            def late_constants():
                nc.gpsimd.iota(expert_no[:, :, :], pattern=[[0, B], [1, E]], base=0,
                               channel_multiplier=0, allow_small_or_imprecise_dtypes=True)\
                    .then_inc(s_eno, 1)
                nc.gpsimd.memset(every[:, :], 1.0).then_inc(s_tri, 1)
                link(nc.gpsimd.memset(before[:, :], 1.0))
                nc.gpsimd.affine_select(out=before[:, :], in_=before[:, :], compare_op=ALU.is_gt,
                                        fill=0.0, base=0, pattern=[[1, NQ]],
                                        channel_multiplier=-1).then_inc(s_tri, 1)

            def rstd(ve, mv, rs):
                pool.wait_ge(s_stat, seen(s_stat))
                link(nc.gpsimd.tensor_scalar(ve[:, :], mv[:, 1:2], EPS, None, ALU.add))
                nc.gpsimd.tensor_tensor(rs[:, :], ve[:, :], half[:, :], ALU.pow).then_inc(s_rstd, 1)

            def step(t, tb):
                if front(t):
                    rstd(ve1, mv1, rs1)
                if t == 0:
                    nc.gpsimd.memset(v_sb[:, :, :, :, HD:32], 1.0).then_inc(s_cact, 1)
                if t == 1:
                    late_constants()
                if front(t):
                    for m in range(2):
                        pool.wait_ge(s_rest, seen(s_rest))
                    link(nc.gpsimd.tensor_copy(parts[:, t % RING, 1, :, :], rest[:, :, :]))
                    nc.gpsimd.tensor_tensor(parts[:, t % RING, 2, :, :], rest[:, :, :],
                                            parts[:, t % RING, 1, :, :], ALU.subtract)\
                        .then_inc(s_parts, 1)
                if attention(t):
                    rstd(ve2, mv2, rs2)

            turns(pool, seen, step)

            pool.wait_ge(s_slot, seen(s_slot))
            pool.wait_ge(s_slotz, seen(s_slotz, 16))
            for b in range(B):
                nc.gpsimd.indirect_dma_start(
                    slots_in, bass.IndirectOffsetOnAxis(ap=slot[:, b:b + 1], axis=0), xn2_sb[:, b, :],
                    None, bounds_check=SLOTS - 1, oob_is_err=False).then_inc(s_scat, 16)
            pool.wait_ge(s_stored, seen(s_stored, 16 * E))
            for b in range(B):
                nc.gpsimd.indirect_dma_start(
                    yt[:, b, :], None, slots_out,
                    bass.IndirectOffsetOnAxis(ap=slot[:, b:b + 1], axis=0),
                    bounds_check=SLOTS - 1, oob_is_err=False).then_inc(s_gath[b], 16)


def kernel(x, ctx_768, g_xattn, g_ffn, L0_xattn_Wq, L0_xattn_bq, L0_xattn_Wk, L0_xattn_bk,
           L0_xattn_Wv, L0_xattn_bv, L0_xattn_Wo, L0_xattn_bo, L0_ffn_wg, L0_ffn_W, L0_ffn_b):
    import numpy as np
    import concourse.bacc as bacc
    from concourse.bass_utils import run_bass_kernel_spmd

    def by_dim(w):
        w = np.asarray(w)
        lead = w.shape[:-1]
        return w.reshape(*lead, H // 2, 2, HD).transpose(*range(len(lead)), -2, -1, -3).reshape(*lead, D)

    arrays = {
        "x": np.asarray(x),
        "ctxT": np.asarray(ctx_768).transpose(2, 0, 1).reshape(2, KC, B, NK),
        "g_xattn": np.asarray(g_xattn), "g_ffn": np.asarray(g_ffn),
        "wq": by_dim(L0_xattn_Wq).reshape(2, 128, D), "bq": by_dim(L0_xattn_bq).reshape(1, D),
        "wk": by_dim(L0_xattn_Wk).reshape(2, KC, D), "bk": by_dim(L0_xattn_bk).reshape(1, D),
        "wv": np.asarray(L0_xattn_Wv).reshape(2, KC, D), "bv": np.asarray(L0_xattn_bv).reshape(1, D),
        "wo": np.asarray(L0_xattn_Wo), "bo": np.asarray(L0_xattn_bo).reshape(1, D),
        "wg": np.asarray(L0_ffn_wg).reshape(2, 128, E),
        "wT": np.asarray(L0_ffn_W).transpose(0, 2, 1).reshape(E, 2, 128, D),
        "be": np.asarray(L0_ffn_b),
    }
    arrays = {f"in_{n}": np.ascontiguousarray(a) for n, a in arrays.items()}
    nc = bacc.Bacc("TRN2", target_bir_lowering=False, num_devices=1)
    args = [nc.dram_tensor(n, a.shape, mybir.dt.from_np(a.dtype), kind="ExternalInput").ap()
            for n, a in arrays.items()]
    args.append(nc.dram_tensor("out", (B, NQ, D), F32, kind="ExternalOutput").ap())
    build(nc, *args)
    return run_bass_kernel_spmd(nc, [arrays], core_ids=[0]).results[0]["out"]
```

```python
from contextlib import ExitStack

import concourse.bass as bass
from concourse import mybir

F32 = mybir.dt.float32
BF16 = mybir.dt.bfloat16
I32 = mybir.dt.int32
ALU = mybir.AluOpType
ACT = mybir.ActivationFunctionType
AX = mybir.AxisListType

B, NQ, D = 8, 112, 256
NK, DC = 375, 192
H, HD = 16, 16
E, CAP = 8, 112
SLOTS = E * CAP
EPS = 1e-5
SCALE = HD ** -0.5
KC = DC // 2
CHUNKS = [(0, 128), (128, 128), (256, NK - 256)]
NCH = len(CHUNKS)
G = H // 4
UNITS = G * NCH
QC = NK
KQ = NK + NQ
K_PART = (0, 0, 0, 1, 1, 2)
Q_PART = (0, 1, 2, 0, 1, 0)
PROD = HD * len(K_PART)
FAR = 4096
RING = 3
FIRST_HEADS = 2
AT_MAXT = 10
AT_ROUTE = 3
EARLY = 3
LAST = B - 1
ROW = 2 * D + 2
X1, GATE, TOKEN = D, 2 * D, 2 * D + 1


def heads_of(unit):
    at = 2 * (unit - FIRST_HEADS)
    return range(max(at, 0), min(at + 2, H))


def build(nc, x, ctxT, gx, gf, wq, bq, wk, bk, wv, bv, wo, bo, wg, wT, be, out):
    slots = nc.dram_tensor("slots", (SLOTS, ROW), F32).ap()
    out_rows = out.rearrange("b n d -> (b n) d")
    with ExitStack() as stack:
        def sb(name, shape, dt=F32):
            return stack.enter_context(nc.sbuf_tensor(name, shape, dt))

        def sem(name):
            return stack.enter_context(nc.semaphore(name))

        wq_sb = sb("wq_sb", [128, 2, D])
        bq_sb = sb("bq_sb", [1, D])
        wk_sb = sb("wk_sb", [KC + 1, 2, D])
        wv_sb = sb("wv_sb", [KC + 1, 2, D])
        wo_sb = sb("wo_sb", [128, G, D])
        wg_sb = sb("wg_sb", [128, 2, E])
        wT_sb = sb("wT_sb", [128, E, 2, D])
        be_sb = sb("be_sb", [NQ, E, D])
        gate_sb = sb("gate_sb", [NQ, 2])
        tanh_sb = sb("tanh_sb", [NQ, 2])
        ident = sb("ident", [128, 128])
        ones_row = sb("ones_row", [1, NQ])
        ones_col = sb("ones_col", [128, 1], BF16)
        half = sb("half", [NQ, B])
        before = sb("before", [NQ, NQ], BF16)
        every = sb("every", [NQ, NQ], BF16)
        expert_no = sb("expert_no", [NQ, B, E])
        x_sb = sb("x_sb", [NQ, B, D])
        rows = sb("rows", [NQ, B, ROW])
        ctx_sb = sb("ctx_sb", [KC + 1, RING, 2, NK])
        st1 = sb("st1", [NQ, B, 6])
        mv1 = sb("mv1", [NQ, B, 2])
        ve1 = sb("ve1", [NQ, B])
        rs1 = sb("rs1", [NQ, B])
        xn = sb("xn", [NQ, B, D])
        xnT = sb("xnT", [128, B, 2, NQ])
        parts = sb("parts", [128, RING, 3, 2, KQ], BF16)
        rest = sb("rest", [128, 2, KQ])
        k6 = sb("k6", [128, RING, H, NK], BF16)
        q6 = sb("q6", [128, RING, H, NQ], BF16)
        v_sb = sb("v_sb", [128, RING, NCH, H, 32])
        nmax = sb("nmax", [NQ, H])
        mparts = sb("mparts", [H, 3, NQ], BF16)
        mrest = sb("mrest", [H, NQ])
        prob = sb("prob", [128, 2, 4 * NQ])
        denT = sb("denT", [128, NQ * G])
        rdenT = sb("rdenT", [128, NQ * G // 32])
        rden = sb("rden", [128, NQ * G])
        onorm = sb("onorm", [128, G, NQ])
        st2 = sb("st2", [NQ, B, 6])
        mv2 = sb("mv2", [NQ, B, 2])
        ve2 = sb("ve2", [NQ, B])
        rs2 = sb("rs2", [NQ, B])
        x2T = sb("x2T", [128, B, 2, NQ])
        lmax = sb("lmax", [NQ, B])
        hit = sb("hit", [NQ, B, E])
        cand = sb("cand", [NQ, B, E])
        idx = sb("idx", [NQ, B])
        maskb = sb("maskb", [NQ, B, E], BF16)
        shifted = sb("shifted", [NQ, B, E])
        expd = sb("expd", [NQ, B, E])
        esum = sb("esum", [NQ, B])
        own = sb("own", [NQ, B, E])
        place = sb("place", [NQ, B])
        kept = sb("kept", [NQ, B])
        slotf = sb("slotf", [NQ, B])
        slot = sb("slot", [NQ, B], I32)
        slot2 = sb("slot2", [NQ, B])
        xin = sb("xin", [CAP, E, ROW])
        xinT, yb, res = xnT, xn, x_sb

        sc = [stack.enter_context(nc.psum_tensor(f"sc{i}", [128, 512], F32)) for i in range(2)]
        stp = [stack.enter_context(nc.psum_tensor(f"stp{i}", [128, 512], F32)) for i in range(2)]
        pj = [stack.enter_context(nc.psum_tensor(f"pj{i}", [128, 512], F32)) for i in range(2)]
        pv = stack.enter_context(nc.psum_tensor("pv", [128, 512], F32))
        misc = stack.enter_context(nc.psum_tensor("misc", [128, 512], F32))

        s_x = sem("first_x_loaded")
        s_xrest = sem("x_rest_loaded")
        s_gate = sem("gates_loaded")
        s_tanh = sem("tanh_ready")
        s_wk = sem("wk_loaded")
        s_wqv = sem("wq_wv_loaded")
        s_wo = sem("wo_loaded")
        s_zeroed = sem("wo_zeroed")
        s_ident = sem("identity_ready")
        s_ones = sem("ones_ready")
        s_pad = sem("rows_96_on_ready")
        s_vones = sem("v_ones_ready")
        s_ctx = sem("ctx_loaded")
        s_stat = sem("variance_ready")
        s_rstd = sem("rstd_ready")
        s_xn = sem("xn_ready")
        s_xnT = sem("xnT_in_psum")
        s_xnTe = sem("xnT_ready")
        s_kq = sem("kq_in_psum")
        s_hi = sem("kq_hi_ready")
        s_rest = sem("kq_rest_ready")
        s_mid = sem("kq_mid_ready")
        s_parts = sem("kq_parts_ready")
        s_first = sem("first_kq_read")
        s_k6 = sem("kq_rows_laid")
        s_v = sem("v_in_psum")
        s_ve = sem("v_ready")
        s_sc = sem("scores_in_psum")
        s_max = sem("max_taken")
        s_mT = sem("maxT_in_psum")
        s_mh = sem("max_hi_ready")
        s_mp = sem("max_parts_ready")
        s_mrow = sem("max_rows_laid")
        s_st = sem("scoresT_in_psum")
        s_p = sem("probs_ready")
        s_pv = sem("pv_in_psum")
        s_on = sem("normalised")
        s_op = sem("wo_product_in_psum")
        s_x1 = sem("x1_ready")
        s_outx = sem("x1_in_out")
        s_xn2 = sem("xn2_ready")
        s_wg = sem("wg_loaded")
        s_wT = sem("experts_loaded")
        s_x2T = sem("x2T_in_psum")
        s_x2Te = sem("x2T_ready")
        s_lg = sem("logits_in_psum")
        s_tri = sem("triangle_ready")
        s_eno = sem("expert_numbers_ready")
        s_mask = sem("mask_ready")
        s_shift = sem("shifted_ready")
        s_exp = sem("router_exp_ready")
        s_place = sem("places_in_psum")
        s_slot = sem("slots_ready")
        s_empty = sem("empty_rows_ready")
        s_cleared = sem("slots_emptied")
        s_scat = sem("tokens_scattered")
        s_xin = [sem(f"expert_{e}_loaded") for e in range(E)]
        s_xinT = sem("xinT_in_psum")
        s_xinTe = sem("xinT_ready")
        s_y = sem("y_in_psum")
        s_yb = sem("y_biased")
        s_be = sem("expert_biases_loaded")
        s_res = sem("result_ready")
        s_out = sem("out_stored")
        s_chain = sem("vector_chain")
        s_pchain = sem("gpsimd_chain")

        class Seen:

            def __init__(self):
                self.n = {}

            def __call__(self, s, more=1):
                had = self.n.get(s.name, (s, 0))[1]
                self.n[s.name] = (s, had + more)
                return had + more

        def settle(eng, seen):
            eng.drain()
            for s, n in seen.n.values():
                eng.sem_inc(s, -n)
            seen.n = {}

        def turns(eng, seen, step):
            for t in range(2):
                step(t, t)
            settle(eng, seen)
            with eng.Fori(0, (B - 2) // RING) as i:
                for k in range(RING):
                    step(2 + k, 2 + k + RING * i)
                settle(eng, seen)
            for t in range(B, B + 2):
                step(t, t)

        def front(t):
            return t < B

        def maxima(t):
            return 1 <= t <= B

        def attention(t):
            return t >= 2

        block = stack.enter_context(nc.Block())

        @block.sync
        def _(sp):
            seen = Seen()
            ctx_b = ctxT.rearrange("c p b n -> p b c n")
            sp.dma_start(wk_sb[0:KC, :, :], wk.rearrange("c p n -> p c n")).then_inc(s_wk, 16)
            sp.dma_start(ctx_sb[0:KC, 0, :, :], ctx_b[:, 0, :, :]).then_inc(s_ctx, 16)
            sp.dma_start(wk_sb[KC:KC + 1, 1, :], bk).then_inc(s_wk, 16)
            sp.dma_start(wq_sb[:, :, :], wq.rearrange("c p n -> p c n")).then_inc(s_wqv, 16)
            sp.dma_start(bq_sb[:, :], bq).then_inc(s_wqv, 16)
            sp.dma_start(wv_sb[0:KC, :, :], wv.rearrange("c p n -> p c n")).then_inc(s_wqv, 16)
            sp.dma_start(wv_sb[KC:KC + 1, 1, :], bv).then_inc(s_wqv, 16)
            sp.dma_start(x_sb[:, 1:B, :], x.rearrange("b p d -> p b d")[:, 1:B, :])\
              .then_inc(s_xrest, 16)

            def step(t, tb):
                if front(t):
                    if t > 0:
                        sp.dma_start(ctx_sb[0:KC, t % RING, :, :],
                                     ctx_b[:, bass.ds(tb, 1), :, :]).then_inc(s_ctx, 16)
                    for part in range(3):
                        sp.wait_ge(s_parts, seen(s_parts))
                        for j in range(len(K_PART)):
                            at = slice(HD * j, HD * (j + 1))
                            if K_PART[j] == part:
                                sp.dma_start(k6[at, t % RING, :, :],
                                             parts[:, t % RING, part, :, 0:NK]).then_inc(s_k6, 16)
                            if Q_PART[j] == part:
                                sp.dma_start(q6[at, t % RING, :, :],
                                             parts[:, t % RING, part, :, QC:KQ]).then_inc(s_k6, 16)
                if t == 1:
                    sp.wait_ge(s_zeroed, seen(s_zeroed))
                    wo_v = wo.rearrange("(a g d) n -> g d a n", g=4, d=HD)
                    for g in range(4):
                        sp.dma_start(wo_sb[32 * g:32 * g + HD, :, :], wo_v[g]).then_inc(s_wo, 16)
                    sp.dma_start(wo_sb[HD:HD + 1, 0, :], bo).then_inc(s_wo, 16)
                    sp.wait_ge(s_empty, seen(s_empty))
                    sp.dma_start(slots.rearrange("(e c) d -> c e d", e=E), xin[:, :, :])\
                      .then_inc(s_cleared, 16)

            turns(sp, seen, step)

            out_v = out.rearrange("b n d -> n b d")
            for lo, hi in ((0, LAST), (LAST, B)):
                sp.wait_ge(s_x1, seen(s_x1))
                sp.dma_start(out_v[:, lo:hi, :], rows[:, lo:hi, X1:X1 + D]).then_inc(s_outx, 16)
            sp.wait_ge(s_scat, seen(s_scat, 16 * B))
            for e in range(E):
                sp.dma_start(xin[:, e, :], slots[e * CAP:(e + 1) * CAP, :]).then_inc(s_xin[e], 16)

        @block.tensor
        def _(pe):
            seen = Seen()
            pe.wait_ge(s_ident, seen(s_ident, 3))

            def turn_xn(lo, hi, bank):
                for b in range(lo, hi):
                    pe.wait_ge(s_xn, seen(s_xn))
                    for c in range(2):
                        at = (2 * (b - lo) + c) * NQ
                        mm = pe.transpose(bank[:, at:at + NQ], xn[:, b, c * 128:(c + 1) * 128],
                                          ident[0:NQ, 0:NQ])
                mm.then_inc(s_xnT, 1)

            def project_kq(t, tb, m):
                cols = slice(m * 128, (m + 1) * 128)
                if m == 0:
                    pe.wait_ge(s_ctx, seen(s_ctx, 16))
                if t > 0:
                    pe.wait_ge(s_ve, seen(s_ve))
                for c in range(2):
                    r = KC + c
                    pe.matmul(pj[m][:, 0:NK], wk_sb[0:r, c, cols], ctx_sb[0:r, t % RING, c, :],
                              start=(c == 0), stop=(c == 1))
                if t == 0 and m == 0:
                    turn_xn(0, 1, misc)
                    pe.wait_ge(s_wqv, seen(s_wqv, 64))
                    pe.wait_ge(s_xnTe, seen(s_xnTe))
                for c in range(2):
                    pe.matmul(pj[m][:, QC:KQ], wq_sb[:, c, cols], xnT[:, bass.ds(tb, 1), c, :],
                              start=(c == 0), stop=False)
                pe.matmul(pj[m][:, QC:KQ], bq_sb[:, cols], ones_row[:, :],
                          start=False, stop=True).then_inc(s_kq, 1)

            def project_v(t, m):
                for n, (k0, kn) in enumerate(CHUNKS):
                    if n // 2 != m:
                        continue
                    for c in range(2):
                        r = KC + c
                        mm = pe.matmul(pj[m][0:kn, (n % 2) * D:(n % 2 + 1) * D],
                                       ctx_sb[0:r, t % RING, c, k0:k0 + kn],
                                       wv_sb[0:r, c, :], start=(c == 0), stop=(c == 1))
                mm.then_inc(s_v, 1)

            def scores(b3, h):
                pe.wait_ge(s_max, seen(s_max))
                pe.matmul(sc[h % 2][0:NQ, 0:NK], q6[0:PROD, b3, h, :], k6[0:PROD, b3, h, :],
                          start=True, stop=True).then_inc(s_sc, 1)

            def scores_T(b3, n):
                g, c = divmod(n, NCH)
                k0, kn = CHUNKS[c]
                for j in range(4):
                    h = 4 * g + j
                    mm = pe.matmul(stp[n % 2][0:kn, j * NQ:(j + 1) * NQ],
                                   k6[:, b3, h, k0:k0 + kn], q6[:, b3, h, :], start=True, stop=True)
                mm.then_inc(s_st, 1)

            def probs_v(b3, n):
                g, c = divmod(n, NCH)
                kn = CHUNKS[c][1]
                pe.wait_ge(s_p, seen(s_p))
                for j in range(4):
                    mm = pe.matmul(pv[32 * j:32 * j + 32, g * NQ:(g + 1) * NQ],
                                   v_sb[0:kn, b3, c, 4 * g + j, :],
                                   prob[0:kn, n % 2, j * NQ:(j + 1) * NQ],
                                   start=(c == 0), stop=(c == NCH - 1), tile_position=(0, 32 * j))
                if n == UNITS - 1:
                    mm.then_inc(s_pv, 1)

            def turn_xn2(b):
                pe.wait_ge(s_xn2, seen(s_xn2))
                for c in range(2):
                    mm = pe.transpose(sc[b % 2][:, c * NQ:(c + 1) * NQ],
                                      rows[:, b, c * 128:(c + 1) * 128], ident[0:NQ, 0:NQ])
                mm.then_inc(s_x2T, 1)

            def logits(b):
                pe.wait_ge(s_x2Te, seen(s_x2Te))
                for c in range(2):
                    mm = pe.matmul(pj[0][0:NQ, b * E:(b + 1) * E], x2T[:, b, c, :], wg_sb[:, c, :],
                                   start=(c == 0), stop=(c == 1))
                if b >= LAST - 1:
                    mm.then_inc(s_lg, 1)

            def places(lo, hi):
                pe.wait_ge(s_mask, seen(s_mask))
                for b in range(hi - 1):
                    at = max(lo, b + 1)
                    pe.matmul(pj[1][0:NQ, (at - lo) * E:(hi - lo) * E], every[:, :],
                              maskb[:, b:b + 1, :].to_broadcast([NQ, hi - at, E]),
                              start=(b == 0), stop=False, skip_group_check=True)
                pe.matmul(pj[1][0:NQ, 0:(hi - lo) * E], before[:, :], maskb[:, lo:hi, :],
                          start=False, stop=True, skip_group_check=True).then_inc(s_place, 1)

            def step(t, tb):
                if t == B:
                    pe.wait_ge(s_ve, seen(s_ve, 2))
                if t == B + 1:
                    pe.wait_ge(s_wg, seen(s_wg, 16))
                    pe.wait_ge(s_tri, seen(s_tri, 2))
                for n in range(UNITS):
                    if front(t) and n < 2:
                        project_kq(t, tb, n)
                    if attention(t):
                        if n == 0:
                            pe.wait_ge(s_mrow, seen(s_mrow, 48))
                        scores_T((t - 2) % RING, n)
                    if maxima(t):
                        if n == FIRST_HEADS:
                            pe.wait_ge(s_k6, seen(s_k6, 16 * 2 * len(K_PART)))
                        for h in heads_of(n):
                            scores((t - 1) % RING, h)
                    if maxima(t) and n == AT_MAXT:
                        pe.wait_ge(s_max, seen(s_max, 0) + 2)
                        pe.transpose(misc[0:H, 0:NQ], nmax[:, :], ident[0:NQ, 0:NQ])\
                          .then_inc(s_mT, 1)
                    if attention(t) and n > 0:
                        probs_v((t - 2) % RING, n - 1)
                    if t == B + 1 and AT_ROUTE <= n < AT_ROUTE + LAST:
                        turn_xn2(n - AT_ROUTE)
                    if t == B + 1 and AT_ROUTE < n <= AT_ROUTE + LAST:
                        logits(n - AT_ROUTE - 1)
                if attention(t):
                    probs_v((t - 2) % RING, UNITS - 1)
                if front(t):
                    if t == 0:
                        pe.wait_ge(s_first, seen(s_first))
                    project_v(t, 0)
                    project_v(t, 1)
                if t == 0:
                    turn_xn(1, 3, sc[0])
                    turn_xn(3, 5, sc[1])
                    turn_xn(5, 7, misc)
                    pe.wait_ge(s_xnTe, seen(s_xnTe))
                    turn_xn(7, 8, sc[0])
                    pe.wait_ge(s_xnTe, seen(s_xnTe, 3))
                if t == 1:
                    pe.wait_ge(s_wo, seen(s_wo, 80))
                    pe.wait_ge(s_pad, seen(s_pad, RING + 1))
                    pe.wait_ge(s_vones, seen(s_vones))
                if t == B + 1:
                    places(0, LAST)
                if attention(t):
                    pe.wait_ge(s_on, seen(s_on))
                    for g in range(G):
                        mm = pe.matmul(misc[0:NQ, 0:D], onorm[:, g, :], wo_sb[:, g, :],
                                       start=(g == 0), stop=(g == G - 1))
                    mm.then_inc(s_op, 1)

            pe.wait_ge(s_wk, seen(s_wk, 32))
            turns(pe, seen, step)
            turn_xn2(LAST)
            logits(LAST)
            places(LAST, B)

            banks = (pj[0], pj[1], stp[0], stp[1])

            def product(e):
                pe.wait_ge(s_xinTe, seen(s_xinTe))
                if e >= len(banks):
                    pe.wait_ge(s_yb, e - len(banks) + 1)
                for c in range(2):
                    mm = pe.matmul(banks[e % len(banks)][0:CAP, 0:D], xinT[:, e, c, :],
                                   wT_sb[:, e, c, :], start=(c == 0), stop=(c == 1))
                mm.then_inc(s_y, 1)

            pe.wait_ge(s_wT, seen(s_wT, 16))
            for e in range(E):
                pe.wait_ge(s_xin[e], 16)
                for c in range(2):
                    mm = pe.transpose(sc[e % 2][:, c * CAP:(c + 1) * CAP],
                                      xin[:, e, c * 128:(c + 1) * 128], ident[0:CAP, 0:CAP])
                mm.then_inc(s_xinT, 1)
                if e:
                    product(e - 1)
            product(E - 1)

        @block.scalar
        def _(act):
            seen = Seen()
            act.dma_start(x_sb[:, 0, :], x[0, :, :]).then_inc(s_x, 16)
            for n, g in enumerate((gx, gf)):
                act.dma_start(gate_sb[:, n:n + 1], g.partition_broadcast(NQ)).then_inc(s_gate, 16)
            act.wait_ge(s_gate, seen(s_gate, 32))
            nc.scalar.activation(tanh_sb[:, :], gate_sb[:, :], ACT.Tanh).then_inc(s_tanh, 1)

            def leave(dst, src, signal):
                nc.scalar.activation(dst, src, ACT.Copy).then_inc(signal, 1)

            def step(t, tb):
                for n in range(UNITS):
                    if t == 0 and n == 0:
                        act.wait_ge(s_xnT, seen(s_xnT))
                        leave(xnT[:, 0, :, :].rearrange("p c n -> p (c n)"), misc[:, 0:2 * NQ], s_xnTe)
                    if front(t) and n < 2:
                        act.wait_ge(s_kq, seen(s_kq))
                        leave(parts[:, t % RING, 0, n, :], pj[n][:, 0:KQ], s_hi)
                    if attention(t):
                        act.wait_ge(s_st, seen(s_st))
                        kn = CHUNKS[n % NCH][1]
                        nc.scalar.activation(prob[0:kn, n % 2, :], stp[n % 2][0:kn, 0:4 * NQ],
                                             ACT.Exp, scale=SCALE).then_inc(s_p, 1)
                    if front(t) and n < 2:
                        act.wait_ge(s_rest, seen(s_rest))
                        if n == 1:
                            act.sem_inc(s_parts, 1)
                        leave(parts[:, t % RING, 1, n, :], rest[:, n, :], s_mid)
                    if maxima(t) and n == AT_MAXT:
                        act.wait_ge(s_mT, seen(s_mT))
                        leave(mparts[:, 0, :], misc[0:H, 0:NQ], s_mh)
                    if t == B + 1 and AT_ROUTE <= n < AT_ROUTE + LAST:
                        b = n - AT_ROUTE
                        act.wait_ge(s_x2T, seen(s_x2T))
                        leave(x2T[:, b, :, :].rearrange("p c n -> p (c n)"), sc[b % 2][:, 0:2 * NQ],
                              s_x2Te)
                if maxima(t):
                    act.wait_ge(s_mp, seen(s_mp))
                    for j in range(3):
                        act.dma_start(q6[PROD + j:PROD + j + 1, (t - 1) % RING, :, :],
                                      mparts[:, j, :]).then_inc(s_mrow, 16)
                if front(t):
                    act.wait_ge(s_v, seen(s_v))
                    leave(v_sb[:, t % RING, 0:2, :, 0:HD],
                          pj[0][:, :].rearrange("p (c h d) -> p c h d", c=2, h=H), s_ve)
                    act.wait_ge(s_v, seen(s_v))
                    kn = CHUNKS[2][1]
                    leave(v_sb[0:kn, t % RING, 2, :, 0:HD],
                          pj[1][0:kn, 0:D].rearrange("p (h d) -> p h d", h=H), s_ve)
                if t == 0:
                    for lo, hi, bank in ((1, 3, sc[0]), (3, 5, sc[1]), (5, 7, misc), (7, 8, sc[0])):
                        act.wait_ge(s_xnT, seen(s_xnT))
                        leave(xnT[:, lo:hi, :, :].rearrange("p b c n -> p (b c n)"),
                              bank[:, 0:2 * (hi - lo) * NQ], s_xnTe)
                    act.wait_ge(s_ones, seen(s_ones))
                    for r in range(RING):
                        nc.scalar.activation(k6[PROD:128, r, :, :].rearrange("p h n -> p (h n)"),
                                             ones_col[PROD:128, :].to_broadcast([128 - PROD, H * NK]),
                                             ACT.Copy).then_inc(s_pad, 1)
                if t == 1:
                    act.dma_start(wg_sb[:, :, :], wg.rearrange("c p e -> p c e")).then_inc(s_wg, 16)
                    act.dma_start(wT_sb[:, :, :, :], wT.rearrange("e c p f -> p e c f"))\
                       .then_inc(s_wT, 16)
                    act.dma_start(be_sb[:, :, :], be.partition_broadcast(NQ)).then_inc(s_be, 16)

            def router_exp(lo, hi):
                act.wait_ge(s_shift, seen(s_shift))
                nc.scalar.activation(expd[:, lo:hi, :], shifted[:, lo:hi, :], ACT.Exp)\
                    .then_inc(s_exp, 1)

            turns(act, seen, step)
            router_exp(0, LAST)
            act.wait_ge(s_x2T, seen(s_x2T))
            leave(x2T[:, LAST, :, :].rearrange("p c n -> p (c n)"), sc[LAST % 2][:, 0:2 * NQ], s_x2Te)
            router_exp(LAST, B)
            for e in range(E):
                act.wait_ge(s_xinT, seen(s_xinT))
                leave(xinT[:, e, :, :].rearrange("p c n -> p (c n)"), sc[e % 2][:, 0:2 * CAP], s_xinTe)

        @block.vector
        def _(dve):
            seen = Seen()

            def link(ins):
                ins.then_inc(s_chain, 1)
                dve.wait_ge(s_chain, seen(s_chain))

            def statistics(lo, hi):
                for b in range(lo, hi):
                    link(nc.vector.bn_stats(st1[:, b, :], x_sb[:, b, :]))
                for b in range(lo, hi):
                    ins = nc.vector.bn_aggr(mv1[:, b, :], st1[:, b, :])
                ins.then_inc(s_stat, 1)

            def normalise(lo, hi):
                dve.wait_ge(s_rstd, seen(s_rstd))
                for b in range(lo, hi):
                    nc.vector.tensor_scalar(xn[:, b, :], x_sb[:, b, :], mv1[:, b, 0:1], rs1[:, b:b + 1],
                                            ALU.subtract, ALU.mult).then_inc(s_xn, 1)

            def route(lo, hi):
                lg = pj[0][0:NQ, lo * E:hi * E].rearrange("p (b e) -> p b e", e=E)
                each = [NQ, hi - lo, E]
                dve.wait_ge(s_lg, seen(s_lg))
                link(nc.vector.tensor_reduce(lmax[:, lo:hi], lg, axis=AX.X, op=ALU.max))
                top = lmax[:, lo:hi].unsqueeze(2).to_broadcast(each)
                nc.vector.tensor_tensor(shifted[:, lo:hi, :], lg, top, ALU.subtract)\
                    .then_inc(s_shift, 1)
                link(nc.vector.tensor_tensor(hit[:, lo:hi, :], lg, top, ALU.is_equal))
                link(nc.vector.scalar_tensor_tensor(cand[:, lo:hi, :], hit[:, lo:hi, :], -float(E),
                                                    expert_no[:, lo:hi, :], ALU.mult, ALU.add))
                link(nc.vector.tensor_reduce(idx[:, lo:hi], cand[:, lo:hi, :], axis=AX.X, op=ALU.min))
                nc.vector.tensor_tensor(maskb[:, lo:hi, :], cand[:, lo:hi, :],
                                        idx[:, lo:hi].unsqueeze(2).to_broadcast(each), ALU.is_equal)\
                    .then_inc(s_mask, 1)

            def assign(lo, hi):
                dve.wait_ge(s_place, seen(s_place))
                before_me = pj[1][0:NQ, 0:(hi - lo) * E].rearrange("p (b e) -> p b e", e=E)
                link(nc.vector.tensor_tensor(own[:, lo:hi, :], before_me, maskb[:, lo:hi, :], ALU.mult))
                link(nc.vector.tensor_reduce(place[:, lo:hi], own[:, lo:hi, :], axis=AX.X, op=ALU.add))
                link(nc.vector.tensor_scalar(kept[:, lo:hi], place[:, lo:hi], float(CAP), None,
                                             ALU.is_lt))
                link(nc.vector.scalar_tensor_tensor(slotf[:, lo:hi], idx[:, lo:hi], float(CAP),
                                                    place[:, lo:hi], ALU.mult, ALU.add))
                link(nc.vector.scalar_tensor_tensor(slot2[:, lo:hi], kept[:, lo:hi], -float(FAR),
                                                    slotf[:, lo:hi], ALU.mult, ALU.add))
                dve.wait_ge(s_exp, seen(s_exp))
                link(nc.vector.tensor_reduce(esum[:, lo:hi], expd[:, lo:hi, :], axis=AX.X, op=ALU.add))
                link(nc.vector.reciprocal(esum[:, lo:hi], esum[:, lo:hi]))
                nc.vector.tensor_scalar(rows[:, lo:hi, GATE], esum[:, lo:hi], tanh_sb[:, 1:2], None,
                                        ALU.mult)
                nc.vector.tensor_scalar(slot[:, lo:hi], slot2[:, lo:hi], float(FAR + E * CAP), None,
                                        ALU.add).then_inc(s_slot, 1)

            def statistics_2(lo, hi):
                for b in range(lo, hi):
                    ins = nc.vector.bn_aggr(mv2[:, b, :], st2[:, b, :])
                ins.then_inc(s_stat, 1)

            def normalise_2(lo, hi):
                dve.wait_ge(s_rstd, seen(s_rstd))
                for b in range(lo, hi):
                    nc.vector.tensor_scalar(rows[:, b, 0:D], rows[:, b, X1:X1 + D], mv2[:, b, 0:1],
                                            rs2[:, b:b + 1], ALU.subtract, ALU.mult).then_inc(s_xn2, 1)

            nc.vector.memset(ones_row[:, :], 1.0).then_inc(s_ident, 1)
            nc.vector.memset(ctx_sb[KC:KC + 1, :, 1, :], 1.0).then_inc(s_ident, 1)
            dve.sem_inc(s_max, 2)
            dve.wait_ge(s_x, seen(s_x, 16))
            statistics(0, 1)
            link(nc.vector.memset(ones_col[:, :], 0.0))
            nc.vector.memset(ones_col[PROD:PROD + 3, :], 1.0).then_inc(s_ones, 1)
            normalise(0, 1)

            def step(t, tb):
                if t == B + 1:
                    dve.drain().then_inc(s_x1, 1)
                    statistics_2(0, LAST)
                    normalise_2(0, LAST)
                for n in range(UNITS):
                    if maxima(t):
                        for h in heads_of(n):
                            dve.wait_ge(s_sc, seen(s_sc))
                            nc.vector.tensor_reduce(nmax[:, h:h + 1], sc[h % 2][0:NQ, 0:NK], axis=AX.X,
                                                    op=ALU.max, negate=True).then_inc(s_max, 1)
                    if front(t) and n < 2:
                        dve.wait_ge(s_hi, seen(s_hi))
                        nc.vector.tensor_tensor(rest[:, n, :], pj[n][:, 0:KQ],
                                                parts[:, t % RING, 0, n, :], ALU.subtract)\
                            .then_inc(s_rest, 1)
                    if maxima(t) and n == AT_MAXT:
                        dve.wait_ge(s_mh, seen(s_mh))
                        link(nc.vector.tensor_tensor(mrest[:, :], misc[0:H, 0:NQ], mparts[:, 0, :],
                                                     ALU.subtract))
                        link(nc.vector.tensor_copy(mparts[:, 1, :], mrest[:, :]))
                        nc.vector.tensor_tensor(mparts[:, 2, :], mrest[:, :], mparts[:, 1, :],
                                                ALU.subtract).then_inc(s_mp, 1)
                if t == 0:
                    dve.drain().then_inc(s_first, 1)
                    dve.wait_ge(s_xrest, seen(s_xrest, 16))
                    statistics(1, B)
                    normalise(1, B)
                    nc.vector.memset(wo_sb[:, :, :], 0.0).then_inc(s_zeroed, 1)
                    nc.vector.memset(q6[PROD:128, :, :, :].bitcast(F32), 0.0).then_inc(s_pad, 1)
                    dve.wait_ge(s_tanh, seen(s_tanh))
                    dve.wait_ge(s_eno, seen(s_eno))
                if t == B + 1:
                    route(0, LAST)
                if attention(t):
                    dve.wait_ge(s_pv, seen(s_pv))
                    link(nc.vector.transpose(denT[:, :], pv[:, 0:G * NQ]))
                    link(nc.vector.reciprocal(rdenT[:, :],
                                              denT[:, :].rearrange("p (k i) -> p k i", i=32)[:, :, HD]))
                    link(nc.vector.transpose(
                        rden[:, :].rearrange("p (k i) -> p k i", i=32),
                        rdenT[:, :].unsqueeze(2).to_broadcast([128, G * NQ // 32, 32])))
                    nc.vector.tensor_tensor(onorm[:, :, :].rearrange("p g n -> p (g n)"),
                                            pv[:, 0:G * NQ], rden[:, :], ALU.mult).then_inc(s_on, 1)
                if t == B + 1:
                    assign(0, LAST)
                if attention(t):
                    dve.wait_ge(s_op, seen(s_op))
                    tok = bass.ds(tb - 2, 1)
                    link(nc.vector.scalar_tensor_tensor(rows[:, tok, X1:X1 + D], misc[0:NQ, 0:D],
                                                        tanh_sb[:, 0:1], x_sb[:, tok, :],
                                                        ALU.mult, ALU.add))
                    link(nc.vector.bn_stats(st2[:, tok, :], rows[:, tok, X1:X1 + D]))

            turns(dve, seen, step)
            statistics_2(LAST, B)
            dve.drain().then_inc(s_x1, 1)
            normalise_2(LAST, B)
            route(LAST, B)
            assign(LAST, B)

            dve.wait_ge(s_be, seen(s_be, 16))
            banks = (pj[0], pj[1], stp[0], stp[1])
            for e in range(E):
                dve.wait_ge(s_y, seen(s_y))
                nc.vector.tensor_tensor(yb[:, e, :], banks[e % 4][0:CAP, 0:D], be_sb[:, e, :], ALU.add)\
                    .then_inc(s_yb, 1)
                dve.wait_ge(s_yb, e + 1)
                nc.vector.scalar_tensor_tensor(res[:, e, :], yb[:, e, :], xin[:, e, GATE:GATE + 1],
                                               xin[:, e, X1:X1 + D], ALU.mult, ALU.add)\
                    .then_inc(s_res, 1)

        @block.gpsimd
        def _(pool):
            seen = Seen()

            def link(ins):
                ins.then_inc(s_pchain, 1)
                pool.wait_ge(s_pchain, seen(s_pchain))

            def rstd(ve, mv, rs, lo, hi):
                pool.wait_ge(s_stat, seen(s_stat))
                link(nc.gpsimd.tensor_scalar(ve[:, lo:hi], mv[:, lo:hi, 1], EPS, None, ALU.add))
                nc.gpsimd.tensor_tensor(rs[:, lo:hi], ve[:, lo:hi], half[:, lo:hi], ALU.pow)\
                    .then_inc(s_rstd, 1)

            def scatter(lo, hi):
                for b in range(lo, hi):
                    nc.gpsimd.indirect_dma_start(
                        slots, bass.IndirectOffsetOnAxis(ap=slot[:, b:b + 1], axis=0), rows[:, b, :],
                        None, bounds_check=SLOTS - 1, oob_is_err=False).then_inc(s_scat, 16)

            link(nc.gpsimd.memset(ident[:, :], 0.0))
            nc.gpsimd.affine_select(out=ident[:, :], in_=ident[:, :], compare_op=ALU.not_equal,
                                    fill=1.0, base=0, pattern=[[-1, 128]],
                                    channel_multiplier=1).then_inc(s_ident, 1)
            link(nc.gpsimd.memset(half[:, :], -0.5))
            rstd(ve1, mv1, rs1, 0, 1)

            def constants():
                nc.gpsimd.memset(v_sb[:, :, :, :, HD:32], 1.0).then_inc(s_vones, 1)
                link(nc.gpsimd.memset(xin[:, :, :], 0.0))
                nc.gpsimd.iota(xin[:, :, TOKEN].bitcast(I32), pattern=[[0, E]], base=FAR,
                               channel_multiplier=0).then_inc(s_empty, 1)
                nc.gpsimd.iota(rows[:, :, TOKEN].bitcast(I32), pattern=[[NQ, B]], base=0,
                               channel_multiplier=1)
                nc.gpsimd.memset(every[:, :], 1.0).then_inc(s_tri, 1)
                link(nc.gpsimd.memset(before[:, :], 1.0))
                nc.gpsimd.affine_select(out=before[:, :], in_=before[:, :], compare_op=ALU.is_gt,
                                        fill=0.0, base=0, pattern=[[1, NQ]],
                                        channel_multiplier=-1).then_inc(s_tri, 1)
                nc.gpsimd.iota(expert_no[:, :, :], pattern=[[0, B], [1, E]], base=0,
                               channel_multiplier=0, allow_small_or_imprecise_dtypes=True)\
                    .then_inc(s_eno, 1)

            def step(t, tb):
                if front(t):
                    for m in range(2):
                        pool.wait_ge(s_mid, seen(s_mid))
                        if m == 1:
                            pool.sem_inc(s_parts, 1)
                        ins = nc.gpsimd.tensor_tensor(parts[:, t % RING, 2, m, :], rest[:, m, :],
                                                      parts[:, t % RING, 1, m, :], ALU.subtract)
                        if m == 0:
                            link(ins)
                    ins.then_inc(s_parts, 1)
                if t == 0:
                    rstd(ve1, mv1, rs1, 1, B)
                    constants()
                if t == B + 1:
                    rstd(ve2, mv2, rs2, 0, LAST)

            turns(pool, seen, step)
            pool.wait_ge(s_slot, seen(s_slot))
            pool.wait_ge(s_cleared, seen(s_cleared, 16))
            scatter(0, EARLY)
            rstd(ve2, mv2, rs2, LAST, B)
            scatter(EARLY, LAST)
            pool.wait_ge(s_slot, seen(s_slot))
            scatter(LAST, B)

            pool.wait_ge(s_outx, seen(s_outx, 32))
            for e in range(E):
                pool.wait_ge(s_res, seen(s_res))
                nc.gpsimd.indirect_dma_start(
                    out_rows, bass.IndirectOffsetOnAxis(
                        ap=xin[:, e, TOKEN:TOKEN + 1].bitcast(I32), axis=0), res[:, e, :],
                    None, bounds_check=B * NQ - 1, oob_is_err=False).then_inc(s_out, 16)
            pool.wait_ge(s_out, seen(s_out, 16 * E))


def kernel(x, ctx_768, g_xattn, g_ffn, L0_xattn_Wq, L0_xattn_bq, L0_xattn_Wk, L0_xattn_bk,
           L0_xattn_Wv, L0_xattn_bv, L0_xattn_Wo, L0_xattn_bo, L0_ffn_wg, L0_ffn_W, L0_ffn_b):
    import numpy as np
    import concourse.bacc as bacc
    from concourse.bass_utils import run_bass_kernel_spmd

    def by_dim(w):
        w = np.asarray(w)
        lead = w.shape[:-1]
        return w.reshape(*lead, H // 2, 2, HD).transpose(*range(len(lead)), -2, -1, -3).reshape(*lead, D)

    arrays = {
        "x": np.asarray(x),
        "ctxT": np.asarray(ctx_768).transpose(2, 0, 1).reshape(2, KC, B, NK),
        "g_xattn": np.asarray(g_xattn), "g_ffn": np.asarray(g_ffn),
        "wq": by_dim(L0_xattn_Wq).reshape(2, 128, D), "bq": by_dim(L0_xattn_bq).reshape(1, D),
        "wk": by_dim(L0_xattn_Wk).reshape(2, KC, D), "bk": by_dim(L0_xattn_bk).reshape(1, D),
        "wv": np.asarray(L0_xattn_Wv).reshape(2, KC, D), "bv": np.asarray(L0_xattn_bv).reshape(1, D),
        "wo": np.asarray(L0_xattn_Wo), "bo": np.asarray(L0_xattn_bo).reshape(1, D),
        "wg": np.asarray(L0_ffn_wg).reshape(2, 128, E),
        "wT": np.asarray(L0_ffn_W).transpose(0, 2, 1).reshape(E, 2, 128, D),
        "be": np.asarray(L0_ffn_b),
    }
    arrays = {f"in_{n}": np.ascontiguousarray(a) for n, a in arrays.items()}
    nc = bacc.Bacc("TRN2", target_bir_lowering=False, num_devices=1)
    args = [nc.dram_tensor(n, a.shape, mybir.dt.from_np(a.dtype), kind="ExternalInput").ap()
            for n, a in arrays.items()]
    args.append(nc.dram_tensor("out", (B, NQ, D), F32, kind="ExternalOutput").ap())
    build(nc, *args)
    return run_bass_kernel_spmd(nc, [arrays], core_ids=[0]).results[0]["out"]
```

```python
from contextlib import ExitStack

import concourse.bass as bass
from concourse import mybir

F32 = mybir.dt.float32
BF16 = mybir.dt.bfloat16
I32 = mybir.dt.int32
ALU = mybir.AluOpType
ACT = mybir.ActivationFunctionType
AX = mybir.AxisListType

B, NQ, D = 8, 112, 256
NK, DC = 375, 192
H, HD = 16, 16
E, CAP = 8, 112
SLOTS = E * CAP
EPS = 1e-5
SCALE = HD ** -0.5
KC = DC // 2
CHUNKS = [(0, 128), (128, 128), (256, NK - 256)]
NCH = len(CHUNKS)
G = H // 4
UNITS = G * NCH
QC = NK
KQ = NK + NQ
K_PART = (0, 0, 0, 1, 1, 2)
Q_PART = (0, 1, 2, 0, 1, 0)
PROD = HD * len(K_PART)
MAXROW = 128 - 3
FAR = 4096
RING = 3
AT_K1, AT_Q1, AT_SPLIT1 = (1, 2), (3, 4), 5
FIRST_HEADS = 1
THREE = 4
AT_V2, AT_V2E = (6, 7), 9
AT_V_OF_1 = (2, 3, 5, 6, 8, 9)
AT_MAXT, AT_MAXT_B = 11, 10
EARLY = 5
NORMED = ((0, B - 2), (B - 2, B - 1), (B - 1, B))
ROUTED = ((0, B - 1), (B - 1, B))
AT_STAT2, AT_NORM2, AT_TURN2 = 2, (5, 6, 7), (6, 7, 8)
AT_X1, AT_NORM6, AT_TURN3, AT_ROUTE, AT_PLACES = 1, 3, (2, 3, 4, 6), 8, 9
ROW = 2 * D + 2
X1, GATE, TOKEN = D, 2 * D, 2 * D + 1


def heads_of(unit):
    at = 2 * (unit - FIRST_HEADS)
    return range(max(at, 0), min(at + 2, H))


def build(nc, x, ctxT, gx, gf, wq, bq, wk, wv, wo, bo, wg, wT, be, out):
    slots = nc.dram_tensor("slots", (SLOTS, ROW), F32).ap()
    out_rows = out.rearrange("b n d -> (b n) d")
    with ExitStack() as stack:
        def sb(name, shape, dt=F32):
            return stack.enter_context(nc.sbuf_tensor(name, shape, dt))

        def sem(name):
            return stack.enter_context(nc.semaphore(name))

        wq_sb = sb("wq_sb", [128, 2, D])
        bq_sb = sb("bq_sb", [1, D])
        wk_sb = sb("wk_sb", [128, 2, D])
        wv_sb = sb("wv_sb", [128, 2, D])
        wo_sb = sb("wo_sb", [128, 2, D])
        bo_sb = sb("bo_sb", [NQ, D])
        tbo = sb("tbo", [NQ, D])
        wg_sb = sb("wg_sb", [128, 2, E])
        wT_sb = sb("wT_sb", [128, E, 2, D])
        be_sb = sb("be_sb", [NQ, E, D])
        gate_sb = sb("gate_sb", [NQ, 2])
        tanh_sb = sb("tanh_sb", [NQ, 2])
        ident = sb("ident", [128, 128])
        ident_b = sb("ident_b", [NQ, NQ], BF16)
        ones_row = sb("ones_row", [1, NQ])
        k_pad = sb("k_pad", [128, NK], BF16)
        half = sb("half", [NQ, B])
        before = sb("before", [NQ, NQ], BF16)
        every = sb("every", [NQ, NQ], BF16)
        expert_no = sb("expert_no", [NQ, B, E])
        x_sb = sb("x_sb", [NQ, B, D])
        rows = sb("rows", [NQ, B, ROW])
        ctx_sb = sb("ctx_sb", [128, RING, 2, NK])
        st1 = sb("st1", [NQ, B, 6])
        mv1 = sb("mv1", [NQ, B, 2])
        ve1 = sb("ve1", [NQ, B])
        rs1 = sb("rs1", [NQ, B])
        xn = sb("xn", [NQ, B, D])
        xnT = sb("xnT", [128, B, 2, NQ])
        parts = sb("parts", [128, RING, 3, 2, KQ], BF16)
        rest = sb("rest", [128, 2, KQ])
        k6 = sb("k6", [128, RING, H, NK], BF16)
        q6 = sb("q6", [128, RING, H, NQ], BF16)
        v_sb = sb("v_sb", [128, RING, NCH, H, 32])
        nmax = sb("nmax", [NQ, H])
        mrest = sb("mrest", [NQ, H])
        mparts = sb("mparts", [NQ, 3, H], BF16)
        mrows = sb("mrows", [3 * H, NQ], BF16)
        prob = sb("prob", [128, 3, 4 * NQ])
        pvT = sb("pvT", [128, NQ * G])
        rden = sb("rden", [128, NQ * G // 32])
        onT = sb("onT", [128, NQ * 2])
        onorm = sb("onorm", [128, 2, NQ])
        st2 = sb("st2", [NQ, B, 6])
        mv2 = sb("mv2", [NQ, B, 2])
        ve2 = sb("ve2", [NQ, B])
        rs2 = sb("rs2", [NQ, B])
        mrs2 = sb("mrs2", [NQ, B])
        nmean = sb("nmean", [NQ, B])
        x2T = sb("x2T", [128, B, 2, NQ])
        lmax = sb("lmax", [NQ, B])
        hit = sb("hit", [NQ, B, E])
        cand = sb("cand", [NQ, B, E])
        idx = sb("idx", [NQ, B])
        maskb = sb("maskb", [NQ, B, E], BF16)
        shifted = sb("shifted", [NQ, B, E])
        expd = sb("expd", [NQ, B, E])
        esum = sb("esum", [NQ, B])
        own = sb("own", [NQ, B, E])
        place = sb("place", [NQ, B])
        first = sb("first", [NQ, B])
        lost = sb("lost", [NQ, B])
        slotf = sb("slotf", [NQ, B])
        slot = sb("slot", [NQ, B], I32)
        xin = sb("xin", [CAP, E, ROW])
        xinT, yb, res = xnT, xn, x_sb

        sc = [stack.enter_context(nc.psum_tensor(f"sc{i}", [128, 512], F32)) for i in range(2)]
        stp = [stack.enter_context(nc.psum_tensor(f"stp{i}", [128, 512], F32)) for i in range(2)]
        pj = [stack.enter_context(nc.psum_tensor(f"pj{i}", [128, 512], F32)) for i in range(2)]
        pv = stack.enter_context(nc.psum_tensor("pv", [128, 512], F32))
        misc = stack.enter_context(nc.psum_tensor("misc", [128, 512], F32))

        s_x = sem("first_x_loaded")
        s_xrest = sem("x_rest_loaded")
        s_gate = sem("gates_loaded")
        s_tanh = sem("tanh_ready")
        s_wk = sem("wk_loaded")
        s_wq = sem("wq_loaded")
        s_wv = sem("wv_loaded")
        s_wo = sem("wo_loaded")
        s_bo = sem("bo_loaded")
        s_tbo = sem("bo_times_tanh_ready")
        s_xbo = sem("bo_added_to_x")
        s_ident = sem("identity_ready")
        s_kpad = sem("k_pad_ready")
        s_pad = sem("rows_96_on_ready")
        s_vones = sem("v_ones_ready")
        s_ctx = sem("ctx_loaded")
        s_ctx1 = sem("ctx_1_loaded")
        s_stat = sem("variance_ready")
        s_rstd = sem("rstd_ready")
        s_xn = sem("xn_ready")
        s_xnT = sem("xnT_in_psum")
        s_xnTe = sem("xnT_ready")
        s_kq = sem("kq_in_psum")
        s_hi = sem("kq_hi_ready")
        s_rest = sem("kq_rest_ready")
        s_mid = sem("kq_mid_ready")
        s_parts = sem("kq_parts_ready")
        s_lo = sem("rest_used")
        s_first = sem("first_kq_read")
        s_k6 = sem("kq_rows_laid")
        s_k60 = sem("kq_rows_of_0_laid")
        s_v = sem("v_in_psum")
        s_ve = sem("v_ready")
        s_sc = sem("scores_in_psum")
        s_max = sem("max_taken")
        s_mp = sem("max_parts_ready")
        s_mT = sem("max_parts_in_psum")
        s_mrows = sem("max_rows_ready")
        s_lastrows = sem("last_max_rows_ready")
        s_identv = sem("identity_for_dve")
        s_mrow = sem("max_rows_laid")
        s_st = sem("scoresT_in_psum")
        s_p = sem("probs_ready")
        s_pv = sem("pv_in_psum")
        s_on = sem("normalised")
        s_op = sem("wo_product_in_psum")
        s_x1 = sem("x1_ready")
        s_outx = sem("x1_in_out")
        s_xn2a = sem("xn2_of_0_to_2_ready")
        s_xn2 = sem("xn2_ready")
        s_nmean = sem("first_rstd_ready")
        s_wg = sem("wg_loaded")
        s_wT = sem("experts_loaded")
        s_x2T = sem("x2T_in_psum")
        s_x2Te = sem("x2T_ready")
        s_lg = sem("logits_in_psum")
        s_tri = sem("triangle_ready")
        s_eno = sem("expert_numbers_ready")
        s_mask = sem("mask_ready")
        s_shift = sem("shifted_ready")
        s_exp = sem("router_exp_ready")
        s_place = sem("places_in_psum")
        s_slot = sem("slots_ready")
        s_empty = sem("empty_rows_ready")
        s_cleared = sem("slots_emptied")
        s_scat = sem("tokens_scattered")
        s_xin = [sem(f"expert_{e}_loaded") for e in range(E)]
        s_xinT = sem("xinT_in_psum")
        s_xinTe = sem("xinT_ready")
        s_y = sem("y_in_psum")
        s_yb = sem("bias_added")
        s_free = sem("product_read")
        s_be = sem("expert_biases_loaded")
        s_res = sem("result_ready")
        s_out = sem("out_stored")
        s_chain = sem("vector_chain")
        s_pchain = sem("gpsimd_chain")

        class Seen:

            def __init__(self):
                self.n, self.base = {}, {}

            def start_turn(self):
                self.base = dict(self.n)

            def __call__(self, s, more=1):
                had = self.n.get(s.name, (s, 0))[1]
                self.n[s.name] = (s, had + more)
                return had + more

        def settle(eng, seen):
            eng.drain()
            for name, (s, n) in seen.n.items():
                before_turn = seen.base.get(name, (s, 0))[1]
                if n > before_turn:
                    eng.sem_inc(s, before_turn - n)
            seen.n = {name: seen.base.get(name, (s, 0)) for name, (s, n) in seen.n.items()}

        def turns(eng, seen, step):
            for t in range(2):
                step(t, t)
            seen.start_turn()
            with eng.Fori(0, (B - 2) // RING) as i:
                for k in range(RING):
                    step(2 + k, 2 + k + RING * i)
                settle(eng, seen)
            for t in range(B, B + 2):
                step(t, t)

        def front(t):
            return t < B

        def maxima(t):
            return 1 <= t <= B

        def attention(t):
            return t >= 2

        def bank_of_sT(t, n):
            if n < THREE:
                return stp[n % 2]
            return (stp[0], stp[1], sc[0] if t == B + 1 else misc)[(n - THREE) % 3]

        def sT_at(n):
            if n <= THREE:
                return (n,)
            if n == THREE + 1:
                return (n, n + 1)
            return (n + 1,) if n + 1 < UNITS else ()

        block = stack.enter_context(nc.Block())

        @block.sync
        def _(sp):
            seen = Seen()
            ctx_b = ctxT.rearrange("c p b n -> p b c n")
            sp.dma_start(wk_sb[:, :, :], wk.rearrange("c p n -> p c n")).then_inc(s_wk, 16)
            sp.dma_start(ctx_sb[0:KC, 0, :, :], ctx_b[:, 0, :, :]).then_inc(s_ctx, 16)
            sp.dma_start(wq_sb[:, :, :], wq.rearrange("c p n -> p c n")).then_inc(s_wq, 16)
            sp.dma_start(bq_sb[:, :], bq).then_inc(s_wq, 16)
            sp.dma_start(x_sb[:, 1:B, :], x.rearrange("b p d -> p b d")[:, 1:B, :])\
              .then_inc(s_xrest, 16)
            sp.dma_start(wv_sb[:, :, :], wv.rearrange("c p n -> p c n")).then_inc(s_wv, 16)
            sp.dma_start(ctx_sb[0:KC, 1, :, :], ctx_b[:, 1, :, :]).then_inc(s_ctx1, 16)

            def lay_rows(b, part):
                laid = s_k60 if b == 0 else s_k6
                sp.wait_ge(s_parts, seen(s_parts))
                for j in range(len(K_PART)):
                    at = slice(HD * j, HD * (j + 1))
                    if K_PART[j] == part:
                        sp.dma_start(k6[at, b % RING, :, :],
                                     parts[:, b % RING, part, :, 0:NK]).then_inc(laid, 16)
                    if Q_PART[j] == part:
                        sp.dma_start(q6[at, b % RING, :, :],
                                     parts[:, b % RING, part, :, QC:KQ]).then_inc(laid, 16)

            def step(t, tb):
                if 2 <= t < B:
                    sp.dma_start(ctx_sb[0:KC, t % RING, :, :],
                                 ctx_b[:, bass.ds(tb, 1), :, :]).then_inc(s_ctx, 16)
                if maxima(t):
                    lay_rows(t - 1, 1)
                    lay_rows(t - 1, 2)
                if front(t):
                    lay_rows(t, 0)
                if t == B:
                    sp.wait_ge(s_empty, seen(s_empty))
                    sp.dma_start(slots.rearrange("(e c) d -> c e d", e=E), xin[:, :, :])\
                      .then_inc(s_cleared, 16)
                    sp.wait_ge(s_lastrows, seen(s_lastrows))
                    sp.dma_start(q6[MAXROW:128, (t - 1) % RING, :, :], mrows[:, :]).then_inc(s_mrow, 16)
                    sp.dma_start(be_sb[:, :, :], be.partition_broadcast(NQ)).then_inc(s_be, 16)

            turns(sp, seen, step)

            out_v = out.rearrange("b n d -> n b d")
            for lo, hi in NORMED:
                sp.wait_ge(s_x1, seen(s_x1))
                sp.dma_start(out_v[:, lo:hi, :], rows[:, lo:hi, X1:X1 + D]).then_inc(s_outx, 16)
            sp.wait_ge(s_scat, seen(s_scat, 16 * B))
            for e in range(E):
                sp.dma_start(xin[:, e, :], slots[e * CAP:(e + 1) * CAP, :]).then_inc(s_xin[e], 16)

        @block.tensor
        def _(pe):
            seen = Seen()
            pe.wait_ge(s_ident, seen(s_ident, 4))

            def turn_xn(lo, hi, bank):
                for b in range(lo, hi):
                    pe.wait_ge(s_xn, seen(s_xn))
                    for c in range(2):
                        at = (2 * (b - lo) + c) * NQ
                        mm = pe.transpose(bank[:, at:at + NQ], xn[:, b, c * 128:(c + 1) * 128],
                                          ident[0:NQ, 0:NQ])
                mm.then_inc(s_xnT, 1)

            def project_k(t, m, c):
                if m == 0 and c == 0:
                    ctx = s_ctx1 if t == 1 else s_ctx
                    pe.wait_ge(ctx, seen(ctx, 16))
                    if t > 0:
                        pe.wait_ge(s_ve, seen(s_ve, 2))
                    if t == 1:
                        pe.wait_ge(s_first, seen(s_first))
                pe.matmul(pj[m][:, 0:NK], wk_sb[:, c, m * 128:(m + 1) * 128],
                          ctx_sb[:, t % RING, c, :], start=(c == 0), stop=(c == 1))

            def project_q(t, tb, m, c):
                cols = slice(m * 128, (m + 1) * 128)
                if t == 0 and m == 0 and c == 0:
                    turn_xn(0, 1, misc)
                    pe.wait_ge(s_wq, seen(s_wq, 32))
                if t < 2 and m == 0 and c == 0:
                    pe.wait_ge(s_xnTe, seen(s_xnTe))
                pe.matmul(pj[m][:, QC:KQ], wq_sb[:, c, cols], xnT[:, bass.ds(tb, 1), c, :],
                          start=(c == 0), stop=False)
                if c == 1:
                    pe.matmul(pj[m][:, QC:KQ], bq_sb[:, cols], ones_row[:, :],
                              start=False, stop=True).then_inc(s_kq, 1)

            def project_kq(t, tb, m):
                for c in range(2):
                    project_k(t, m, c)
                for c in range(2):
                    project_q(t, tb, m, c)

            def project_v(t, n, c):
                bank = (stp if t < 2 else pj)[n // 2]
                k0, kn = CHUNKS[n]
                at = (n % 2) * D
                mm = pe.matmul(bank[0:kn, at:at + D], ctx_sb[:, t % RING, c, k0:k0 + kn],
                               wv_sb[:, c, :], start=(c == 0), stop=(c == 1))
                if n > 0 and c == 1:
                    mm.then_inc(s_v, 1)

            def scores(b3, h):
                pe.wait_ge(s_max, seen(s_max))
                pe.matmul(sc[h % 2][0:NQ, 0:NK], q6[0:MAXROW, b3, h, :], k6[0:MAXROW, b3, h, :],
                          start=True, stop=True).then_inc(s_sc, 1)

            def scores_T(t, b3, n):
                g, c = divmod(n, NCH)
                k0, kn = CHUNKS[c]
                for j in range(4):
                    h = 4 * g + j
                    mm = pe.matmul(bank_of_sT(t, n)[0:kn, j * NQ:(j + 1) * NQ],
                                   k6[:, b3, h, k0:k0 + kn], q6[:, b3, h, :], start=True, stop=True)
                mm.then_inc(s_st, 1)

            def probs_v(b3, n):
                g, c = divmod(n, NCH)
                kn = CHUNKS[c][1]
                pe.wait_ge(s_p, seen(s_p))
                for j in range(4):
                    mm = pe.matmul(pv[32 * j:32 * j + 32, g * NQ:(g + 1) * NQ],
                                   v_sb[0:kn, b3, c, 4 * g + j, :],
                                   prob[0:kn, n % 3, j * NQ:(j + 1) * NQ],
                                   start=(c == 0), stop=(c == NCH - 1), tile_position=(0, 32 * j))
                if n == UNITS - 1:
                    mm.then_inc(s_pv, 1)

            def turn_xn2(b):
                ready = s_xn2a if b < len(AT_NORM2) else s_xn2
                pe.wait_ge(ready, seen(ready))
                for c in range(2):
                    mm = pe.transpose(pj[1][:, c * NQ:(c + 1) * NQ],
                                      rows[:, b, c * 128:(c + 1) * 128], ident[0:NQ, 0:NQ])
                mm.then_inc(s_x2T, 1)

            def logits(b):
                pe.wait_ge(s_x2Te, seen(s_x2Te))
                for c in range(2):
                    mm = pe.matmul(pj[0][0:NQ, b * E:(b + 1) * E], x2T[:, b, c, :], wg_sb[:, c, :],
                                   start=(c == 0), stop=(c == 1))
                if b + 1 in (ROUTED[0][1], ROUTED[1][1]):
                    mm.then_inc(s_lg, 1)

            def earlier_tiles(lo, hi):
                for b in range(hi - 1):
                    at = max(lo, b + 1)
                    pe.matmul(sc[1][0:NQ, (at - lo) * E:(hi - lo) * E], every[:, :],
                              maskb[:, b:b + 1, :].to_broadcast([NQ, hi - at, E]),
                              start=(b == 0), stop=False, skip_group_check=True)

            def own_tile(lo, hi):
                pe.matmul(sc[1][0:NQ, 0:(hi - lo) * E], before[:, :], maskb[:, lo:hi, :],
                          start=False, stop=True, skip_group_check=True).then_inc(s_place, 1)

            def lead_in(t, tb):
                project_kq(t, tb, 1)
                if t == 0:
                    pe.wait_ge(s_wv, seen(s_wv, 16))
                    for n in (2, 0, 1):
                        for c in range(2):
                            project_v(t, n, c)
                    turn_xn(1, 3, sc[0])
                    pe.wait_ge(s_ident, seen(s_ident))
                else:
                    turn_xn(3, 5, sc[1])
                    turn_xn(5, 7, misc)
                    turn_xn(7, 8, sc[0])
                    pe.wait_ge(s_xnTe, seen(s_xnTe, 3))

            def through_wo():
                pe.wait_ge(s_on, seen(s_on))
                for g in range(2):
                    mm = pe.matmul(misc[0:NQ, 0:D], onorm[:, g, :], wo_sb[:, g, :],
                                   start=(g == 0), stop=(g == 1))
                mm.then_inc(s_op, 1)

            def step(t, tb):
                if t == B:
                    pe.wait_ge(s_ve, seen(s_ve, 2))
                    pe.wait_ge(s_wg, seen(s_wg, 16))
                    pe.wait_ge(s_tri, seen(s_tri, 2))
                for n in range(UNITS):
                    if front(t) and n == 0:
                        project_kq(t, tb, 0)
                    if t < 2 and n == 0:
                        lead_in(t, tb)
                    if attention(t):
                        if n == 0:
                            pe.wait_ge(s_mrow, seen(s_mrow, 16))
                        for u in sT_at(n):
                            scores_T(t, (t - 2) % RING, u)
                    if maxima(t):
                        if t == 1 and n == FIRST_HEADS:
                            pe.wait_ge(s_pad, seen(s_pad, 33))
                        if n == FIRST_HEADS:
                            laid = s_k60 if t == 1 else s_k6
                            pe.wait_ge(laid, seen(laid, 16 * 2 * len(K_PART)))
                        for h in heads_of(n)[0:1]:
                            scores((t - 1) % RING, h)
                    if 2 <= t < B:
                        if n in AT_K1:
                            project_k(t, 1, AT_K1.index(n))
                        if n in AT_Q1:
                            project_q(t, tb, 1, AT_Q1.index(n))
                        if n in AT_V2:
                            project_v(t, 2, AT_V2.index(n))
                    if t == 1 and n in AT_V_OF_1:
                        project_v(t, (2, 0, 1)[AT_V_OF_1.index(n) // 2], AT_V_OF_1.index(n) % 2)
                    if maxima(t):
                        for h in heads_of(n)[1:]:
                            scores((t - 1) % RING, h)
                    if maxima(t) and n == (AT_MAXT_B if t == B else AT_MAXT):
                        pe.wait_ge(s_mp, seen(s_mp))
                        pe.matmul(sc[0][0:3 * H, 0:NQ], mparts[:, :, :].rearrange("p j h -> p (j h)"),
                                  ident_b[:, :], start=True, stop=True).then_inc(s_mT, 1)
                    if t == B + 1 and n == AT_X1:
                        through_wo()
                    if attention(t) and n > 0:
                        probs_v((t - 2) % RING, n - 1)
                    if t == B:
                        if n - 1 in AT_TURN2:
                            logits(AT_TURN2.index(n - 1))
                        if n in AT_TURN2:
                            turn_xn2(AT_TURN2.index(n))
                    if t == B + 1:
                        if n - 1 in AT_TURN3:
                            logits(3 + AT_TURN3.index(n - 1))
                        if n in AT_TURN3:
                            turn_xn2(3 + AT_TURN3.index(n))
                        if n == AT_PLACES:
                            pe.wait_ge(s_mask, seen(s_mask))
                            earlier_tiles(*ROUTED[0])
                            own_tile(*ROUTED[0])
                if attention(t):
                    probs_v((t - 2) % RING, UNITS - 1)
                if 2 <= t < B:
                    for n in range(2):
                        for c in range(2):
                            project_v(t, n, c)
                if t == 1:
                    pe.wait_ge(s_wo, seen(s_wo, 16))
                    pe.wait_ge(s_vones, seen(s_vones))
                if attention(t) and t != B:
                    through_wo()

            pe.wait_ge(s_wk, seen(s_wk, 16))
            turns(pe, seen, step)
            turn_xn2(B - 1)
            earlier_tiles(*ROUTED[1])
            logits(B - 1)
            pe.wait_ge(s_mask, seen(s_mask))
            own_tile(*ROUTED[1])

            banks = (pj[0], pj[1], stp[0], stp[1])

            def product(e):
                pe.wait_ge(s_xinTe, seen(s_xinTe))
                if e >= len(banks):
                    pe.wait_ge(s_free, seen(s_free))
                for c in range(2):
                    mm = pe.matmul(banks[e % len(banks)][0:CAP, 0:D], xinT[:, e, c, :],
                                   wT_sb[:, e, c, :], start=(c == 0), stop=(c == 1))
                mm.then_inc(s_y, 1)

            pe.wait_ge(s_wT, seen(s_wT, 16))
            for e in range(E):
                pe.wait_ge(s_xin[e], 16)
                for c in range(2):
                    mm = pe.transpose(sc[e % 2][:, c * CAP:(c + 1) * CAP],
                                      xin[:, e, c * 128:(c + 1) * 128], ident[0:CAP, 0:CAP])
                mm.then_inc(s_xinT, 1)
                if e:
                    product(e - 1)
            product(E - 1)

        @block.scalar
        def _(act):
            seen = Seen()
            act.dma_start(x_sb[:, 0, :], x[0, :, :]).then_inc(s_x, 16)
            for n, g in enumerate((gx, gf)):
                act.dma_start(gate_sb[:, n:n + 1], g.partition_broadcast(NQ)).then_inc(s_gate, 16)
            act.dma_start(bo_sb[:, :], bo.partition_broadcast(NQ)).then_inc(s_bo, 16)
            act.dma_start(wo_sb[:, :, :], wo).then_inc(s_wo, 16)
            act.wait_ge(s_kpad, seen(s_kpad))
            heads = RING * H
            for dst, row in ((slice(PROD, MAXROW), PROD + 3), (slice(MAXROW, 128), PROD)):
                rows_n = dst.stop - dst.start
                act.dma_start(k6[dst, :, :, :].rearrange("p r h n -> p (r h) n"),
                              k_pad[row:row + rows_n, :].unsqueeze(1)
                                                        .to_broadcast([rows_n, heads, NK]))\
                   .then_inc(s_pad, 16)
            act.wait_ge(s_gate, seen(s_gate, 32))
            nc.scalar.activation(tanh_sb[:, :], gate_sb[:, :], ACT.Tanh).then_inc(s_tanh, 1)

            def leave(dst, src, signal):
                nc.scalar.activation(dst, src, ACT.Copy).then_inc(signal, 1)

            def leave_hi(t, m):
                act.wait_ge(s_kq, seen(s_kq))
                leave(parts[:, t % RING, 0, m, :], pj[m][:, 0:KQ], s_hi)

            def copy_mid(t, m):
                act.wait_ge(s_rest, seen(s_rest))
                if m == 1:
                    act.sem_inc(s_parts, 1)
                leave(parts[:, t % RING, 1, m, :], rest[:, m, :], s_mid)

            def leave_v2(t):
                act.wait_ge(s_v, seen(s_v))
                kn = CHUNKS[2][1]
                leave(v_sb[0:kn, t % RING, 2, :, 0:HD],
                      (stp if t < 2 else pj)[1][0:kn, 0:D].rearrange("p (h d) -> p h d", h=H), s_ve)

            def leave_v01(t):
                act.wait_ge(s_v, seen(s_v))
                leave(v_sb[:, t % RING, 0:2, :, 0:HD],
                      (stp if t < 2 else pj)[0][:, :].rearrange("p (c h d) -> p c h d", c=2, h=H), s_ve)

            def lay_max_rows(b):
                act.wait_ge(s_mrows, seen(s_mrows))
                act.dma_start(q6[MAXROW:128, b % RING, :, :], mrows[:, :]).then_inc(s_mrow, 16)

            def leave_x2T(b):
                act.wait_ge(s_x2T, seen(s_x2T))
                leave(x2T[:, b, :, :].rearrange("p c n -> p (c n)"), pj[1][:, 0:2 * NQ], s_x2Te)

            def router_exp(lo, hi):
                act.wait_ge(s_shift, seen(s_shift))
                nc.scalar.activation(expd[:, lo:hi, :], shifted[:, lo:hi, :], ACT.Exp)\
                    .then_inc(s_exp, 1)

            XN_TURNS = (((1, 3, sc[0]),), ((3, 5, sc[1]), (5, 7, misc), (7, 8, sc[0])))

            def step(t, tb):
                for n in range(UNITS):
                    if t == 0 and n == 0:
                        act.wait_ge(s_xnT, seen(s_xnT))
                        leave(xnT[:, 0, :, :].rearrange("p c n -> p (c n)"), misc[:, 0:2 * NQ], s_xnTe)
                    if front(t) and n == 0:
                        leave_hi(t, 0)
                    if attention(t):
                        act.wait_ge(s_st, seen(s_st))
                        kn = CHUNKS[n % NCH][1]
                        nc.scalar.activation(prob[0:kn, n % 3, :], bank_of_sT(t, n)[0:kn, 0:4 * NQ],
                                             ACT.Exp, scale=SCALE).then_inc(s_p, 1)
                    if front(t) and n == 0:
                        copy_mid(t, 0)
                    if t == 1 and n == AT_V_OF_1[-1]:
                        leave_v2(t)
                        leave_v01(t)
                    if 2 <= t < B:
                        if n == AT_Q1[1]:
                            leave_hi(t, 1)
                        if n == AT_SPLIT1:
                            copy_mid(t, 1)
                        if n == AT_V2E:
                            leave_v2(t)
                    if t < 2 and n == 0:
                        leave_hi(t, 1)
                        copy_mid(t, 1)
                        if t == 0:
                            leave_v2(t)
                            leave_v01(t)
                        for lo, hi, bank in XN_TURNS[t]:
                            act.wait_ge(s_xnT, seen(s_xnT))
                            leave(xnT[:, lo:hi, :, :].rearrange("p b c n -> p (b c n)"),
                                  bank[:, 0:2 * (hi - lo) * NQ], s_xnTe)
                    if t == 1 and n == 0:
                        act.dma_start(wg_sb[:, :, :], wg.rearrange("c p e -> p c e")).then_inc(s_wg, 16)
                    if t == B and n == 0:
                        act.dma_start(wT_sb[:, :, :, :], wT.rearrange("e c p f -> p e c f"))\
                           .then_inc(s_wT, 16)
                    if maxima(t) and n == (AT_MAXT_B if t == B else AT_MAXT):
                        act.wait_ge(s_mT, seen(s_mT))
                        leave(mrows[:, :], sc[0][0:3 * H, 0:NQ], s_lastrows if t == B else s_mrows)
                    if t == B and n in AT_TURN2:
                        leave_x2T(AT_TURN2.index(n))
                    if t == B and n in AT_NORM2:
                        b = AT_NORM2.index(n)
                        if b == 0:
                            act.wait_ge(s_nmean, seen(s_nmean))
                        nc.scalar.activation(rows[:, b, 0:D], rows[:, b, X1:X1 + D], ACT.Identity,
                                             bias=nmean[:, b:b + 1], scale=rs2[:, b:b + 1])\
                            .then_inc(s_xn2a, 1)
                    if t == B + 1 and n in AT_TURN3:
                        leave_x2T(3 + AT_TURN3.index(n))
                    if t == B + 1 and n == AT_ROUTE:
                        router_exp(*ROUTED[0])
                if maxima(t) and t != B:
                    lay_max_rows(t - 1)
                if 2 <= t < B:
                    leave_v01(t)

            turns(act, seen, step)
            leave_x2T(B - 1)
            router_exp(*ROUTED[1])
            for e in range(E):
                act.wait_ge(s_xinT, seen(s_xinT))
                leave(xinT[:, e, :, :].rearrange("p c n -> p (c n)"), sc[e % 2][:, 0:2 * CAP], s_xinTe)

        @block.vector
        def _(dve):
            seen = Seen()

            def link(ins):
                ins.then_inc(s_chain, 1)
                dve.wait_ge(s_chain, seen(s_chain))

            def statistics(lo, hi):
                for b in range(lo, hi):
                    link(nc.vector.bn_stats(st1[:, b, :], x_sb[:, b, :]))
                for b in range(lo, hi):
                    ins = nc.vector.bn_aggr(mv1[:, b, :], st1[:, b, :])
                ins.then_inc(s_stat, 1)

            def normalise(lo, hi):
                dve.wait_ge(s_rstd, seen(s_rstd))
                for b in range(lo, hi):
                    nc.vector.tensor_scalar(xn[:, b, :], x_sb[:, b, :], mv1[:, b, 0:1], rs1[:, b:b + 1],
                                            ALU.subtract, ALU.mult).then_inc(s_xn, 1)

            def route(lo, hi):
                lg = pj[0][0:NQ, lo * E:hi * E].rearrange("p (b e) -> p b e", e=E)
                each = [NQ, hi - lo, E]
                dve.wait_ge(s_lg, seen(s_lg))
                link(nc.vector.tensor_reduce(lmax[:, lo:hi], lg, axis=AX.X, op=ALU.max))
                top = lmax[:, lo:hi].unsqueeze(2).to_broadcast(each)
                nc.vector.tensor_tensor(shifted[:, lo:hi, :], lg, top, ALU.subtract)\
                    .then_inc(s_shift, 1)
                link(nc.vector.tensor_tensor(hit[:, lo:hi, :], lg, top, ALU.is_equal))
                nc.vector.scalar_tensor_tensor(cand[:, lo:hi, :], hit[:, lo:hi, :], -float(E),
                                               expert_no[:, lo:hi, :], ALU.mult, ALU.add)
                dve.wait_ge(s_exp, seen(s_exp))
                link(nc.vector.tensor_reduce(esum[:, lo:hi], expd[:, lo:hi, :], axis=AX.X, op=ALU.add))
                nc.vector.tensor_reduce(idx[:, lo:hi], cand[:, lo:hi, :], axis=AX.X, op=ALU.min)
                link(nc.vector.reciprocal(esum[:, lo:hi], esum[:, lo:hi]))
                nc.vector.tensor_tensor(maskb[:, lo:hi, :], cand[:, lo:hi, :],
                                        idx[:, lo:hi].unsqueeze(2).to_broadcast(each), ALU.is_equal)\
                    .then_inc(s_mask, 1)
                nc.vector.tensor_scalar(rows[:, lo:hi, GATE], esum[:, lo:hi], tanh_sb[:, 1:2], None,
                                        ALU.mult)

            def assign(lo, hi):
                nc.vector.tensor_scalar(first[:, lo:hi], idx[:, lo:hi], float(E), float(CAP),
                                        ALU.add, ALU.mult)
                dve.wait_ge(s_place, seen(s_place))
                before_me = sc[1][0:NQ, 0:(hi - lo) * E].rearrange("p (b e) -> p b e", e=E)
                link(nc.vector.tensor_tensor(own[:, lo:hi, :], before_me, maskb[:, lo:hi, :], ALU.mult))
                link(nc.vector.tensor_reduce(place[:, lo:hi], own[:, lo:hi, :], axis=AX.X, op=ALU.add))
                nc.vector.tensor_scalar(lost[:, lo:hi], place[:, lo:hi], float(CAP), float(FAR),
                                        ALU.is_ge, ALU.mult)
                link(nc.vector.tensor_tensor(slotf[:, lo:hi], first[:, lo:hi], place[:, lo:hi], ALU.add))
                nc.vector.tensor_tensor(slot[:, lo:hi], slotf[:, lo:hi], lost[:, lo:hi], ALU.add)\
                    .then_inc(s_slot, 1)

            def statistics_2(lo, hi):
                for b in range(lo, hi):
                    ins = nc.vector.bn_aggr(mv2[:, b, :], st2[:, b, :])
                ins.then_inc(s_stat, 1)

            def normalise_2(b):
                nc.vector.tensor_scalar(rows[:, b, 0:D], rows[:, b, X1:X1 + D], mv2[:, b, 0:1],
                                        rs2[:, b:b + 1], ALU.subtract, ALU.mult).then_inc(s_xn2, 1)

            def add_x(b):
                dve.wait_ge(s_op, seen(s_op))
                tok = bass.ds(b, 1)
                link(nc.vector.scalar_tensor_tensor(rows[:, tok, X1:X1 + D], misc[0:NQ, 0:D],
                                                    tanh_sb[:, 0:1], x_sb[:, tok, :],
                                                    ALU.mult, ALU.add))
                link(nc.vector.bn_stats(st2[:, tok, :], rows[:, tok, X1:X1 + D]))

            nc.vector.memset(ctx_sb[KC:128, 0, :, :], 1.0).then_inc(s_ident, 1)
            nc.vector.memset(ones_row[:, :], 1.0).then_inc(s_ident, 1)
            dve.sem_inc(s_max, 2)
            dve.wait_ge(s_identv, seen(s_identv))
            nc.vector.tensor_copy(ident_b[:, :], ident[0:NQ, 0:NQ]).then_inc(s_ident, 1)
            dve.wait_ge(s_x, seen(s_x, 16))
            statistics(0, 1)
            normalise(0, 1)

            def split(t, m):
                dve.wait_ge(s_hi, seen(s_hi))
                if t > 0 and m == 0:
                    dve.wait_ge(s_lo, seen(s_lo))
                nc.vector.tensor_tensor(rest[:, m, :], pj[m][:, 0:KQ],
                                        parts[:, t % RING, 0, m, :], ALU.subtract)\
                    .then_inc(s_rest, 1)

            def step(t, tb):
                for n in range(UNITS):
                    if maxima(t):
                        for h in heads_of(n):
                            dve.wait_ge(s_sc, seen(s_sc))
                            nc.vector.tensor_reduce(nmax[:, h:h + 1], sc[h % 2][0:NQ, 0:NK], axis=AX.X,
                                                    op=ALU.max, negate=True).then_inc(s_max, 1)
                    if front(t) and n == 0:
                        split(t, 0)
                    if t == 0 and n == 0:
                        dve.wait_ge(s_xrest, seen(s_xrest, 16))
                        statistics(1, 3)
                    if front(t) and n == (0 if t < 2 else AT_Q1[1]):
                        split(t, 1)
                    if t == 0 and n == 0:
                        dve.drain().then_inc(s_first, 1)
                        normalise(1, 3)
                        statistics(3, B)
                        normalise(3, B)
                    if t == B and n == AT_STAT2:
                        dve.drain().then_inc(s_x1, 1)
                        statistics_2(*NORMED[0])
                    if t == B + 1 and n == AT_X1:
                        add_x(B - 2)
                        dve.drain().then_inc(s_x1, 1)
                        statistics_2(*NORMED[1])
                    if t == B + 1 and n == AT_NORM6:
                        dve.wait_ge(s_rstd, seen(s_rstd))
                        normalise_2(B - 2)
                    if t == B + 1 and n == AT_ROUTE:
                        route(*ROUTED[0])
                    if t == B + 1 and n == AT_PLACES:
                        assign(*ROUTED[0])
                    if maxima(t) and n == (AT_MAXT_B if t == B else AT_MAXT):
                        dve.drain()
                        link(nc.vector.tensor_copy(mparts[:, 0, :], nmax[:, :]))
                        link(nc.vector.tensor_tensor(mrest[:, :], nmax[:, :], mparts[:, 0, :],
                                                     ALU.subtract))
                        link(nc.vector.tensor_copy(mparts[:, 1, :], mrest[:, :]))
                        nc.vector.tensor_tensor(mparts[:, 2, :], mrest[:, :], mparts[:, 1, :],
                                                ALU.subtract).then_inc(s_mp, 1)
                    if t == B and n == AT_MAXT_B:
                        dve.wait_ge(s_rstd, seen(s_rstd))
                        for b in range(len(AT_NORM2), B - 2):
                            normalise_2(b)
                if t == 0:
                    dve.wait_ge(s_tanh, seen(s_tanh))
                    dve.wait_ge(s_bo, seen(s_bo, 16))
                    nc.vector.tensor_scalar(tbo[:, :], bo_sb[:, :], tanh_sb[:, 0:1], None, ALU.mult)\
                        .then_inc(s_tbo, 1)
                if t == 1:
                    dve.wait_ge(s_xbo, seen(s_xbo))
                    dve.wait_ge(s_eno, seen(s_eno))
                if attention(t):
                    dve.wait_ge(s_pv, seen(s_pv))
                    blocks = NQ * G // 32
                    turned = pvT[:, :].rearrange("p (k i) -> p k i", i=32)
                    link(nc.vector.transpose(pvT[:, :], pv[:, 0:G * NQ]))
                    link(nc.vector.reciprocal(rden[:, :], turned[:, :, HD]))
                    link(nc.vector.tensor_tensor(
                        onT[:, :].rearrange("p (k s d) -> p s k d", s=2, d=HD),
                        pvT[:, :].rearrange("p (s k i) -> p s k i", s=2, i=32)[:, :, :, 0:HD],
                        rden[:, :].rearrange("p (s k) -> p s k", s=2).unsqueeze(3)
                                  .to_broadcast([128, 2, blocks // 2, HD]), ALU.mult))
                    nc.vector.transpose(onorm[:, :, :].rearrange("p g n -> p (g n)"), onT[:, :])\
                        .then_inc(s_on, 1)
                if attention(t) and t != B:
                    add_x(tb - 2)

            turns(dve, seen, step)
            statistics_2(*NORMED[2])
            dve.wait_ge(s_rstd, seen(s_rstd))
            normalise_2(B - 1)
            dve.drain().then_inc(s_x1, 1)
            route(*ROUTED[1])
            assign(*ROUTED[1])

            dve.wait_ge(s_be, seen(s_be, 16))
            banks = (pj[0], pj[1], stp[0], stp[1])

            def add_bias(e):
                dve.wait_ge(s_xin[e], 16)
                nc.vector.scalar_tensor_tensor(yb[:, e, :], be_sb[:, e, :], xin[:, e, GATE:GATE + 1],
                                               xin[:, e, X1:X1 + D], ALU.mult, ALU.add)\
                    .then_inc(s_yb, 1)

            add_bias(0)
            for e in range(E):
                if e + 1 < E:
                    add_bias(e + 1)
                dve.wait_ge(s_yb, e + 1)
                dve.wait_ge(s_y, seen(s_y))
                nc.vector.scalar_tensor_tensor(res[:, e, :], banks[e % 4][0:CAP, 0:D],
                                               xin[:, e, GATE:GATE + 1], yb[:, e, :],
                                               ALU.mult, ALU.add).then_inc(s_res, 1)

        @block.gpsimd
        def _(pool):
            seen = Seen()

            def link(ins):
                ins.then_inc(s_pchain, 1)
                pool.wait_ge(s_pchain, seen(s_pchain))

            def rstd(ve, mv, rs, lo, hi, signal=s_rstd):
                pool.wait_ge(s_stat, seen(s_stat))
                link(nc.gpsimd.tensor_scalar(ve[:, lo:hi], mv[:, lo:hi, 1], EPS, None, ALU.add))
                nc.gpsimd.tensor_tensor(rs[:, lo:hi], ve[:, lo:hi], half[:, lo:hi], ALU.pow)\
                    .then_inc(signal, 1)

            def scatter(lo, hi):
                for b in range(lo, hi):
                    nc.gpsimd.indirect_dma_start(
                        slots, bass.IndirectOffsetOnAxis(ap=slot[:, b:b + 1], axis=0), rows[:, b, :],
                        None, bounds_check=SLOTS - 1, oob_is_err=False).then_inc(s_scat, 16)

            link(nc.gpsimd.memset(ident[:, :], 0.0))
            nc.gpsimd.affine_select(out=ident[:, :], in_=ident[:, :], compare_op=ALU.not_equal,
                                    fill=1.0, base=0, pattern=[[-1, 128]],
                                    channel_multiplier=1).then_inc(s_ident, 1)
            link(nc.gpsimd.memset(half[:, :], -0.5))
            pool.sem_inc(s_identv, 1)
            link(nc.gpsimd.memset(k_pad[PROD:128, :], 0.0))
            link(nc.gpsimd.memset(k_pad[PROD:PROD + 3, :], 1.0))
            pool.sem_inc(s_kpad, 1)
            rstd(ve1, mv1, rs1, 0, 1)
            pool.drain()
            nc.gpsimd.memset(ctx_sb[KC:128, 1:RING, :, :], 1.0).then_inc(s_ident, 1)
            nc.gpsimd.memset(q6[PROD:128, :, :, :].bitcast(F32), 0.0).then_inc(s_pad, 1)
            pool.drain()

            def constants():
                nc.gpsimd.memset(v_sb[:, :, :, :, HD:32], 1.0).then_inc(s_vones, 1)
                link(nc.gpsimd.memset(xin[:, :, :], 0.0))
                nc.gpsimd.iota(xin[:, :, TOKEN].bitcast(I32), pattern=[[0, E]], base=FAR,
                               channel_multiplier=0).then_inc(s_empty, 1)
                nc.gpsimd.iota(rows[:, :, TOKEN].bitcast(I32), pattern=[[NQ, B]], base=0,
                               channel_multiplier=1)
                nc.gpsimd.memset(every[:, :], 1.0).then_inc(s_tri, 1)
                link(nc.gpsimd.memset(before[:, :], 1.0))
                nc.gpsimd.affine_select(out=before[:, :], in_=before[:, :], compare_op=ALU.is_gt,
                                        fill=0.0, base=0, pattern=[[1, NQ]],
                                        channel_multiplier=-1).then_inc(s_tri, 1)
                nc.gpsimd.iota(expert_no[:, :, :], pattern=[[0, B], [1, E]], base=0,
                               channel_multiplier=0, allow_small_or_imprecise_dtypes=True)\
                    .then_inc(s_eno, 1)

            def step(t, tb):
                if front(t):
                    for m in range(2):
                        pool.wait_ge(s_mid, seen(s_mid))
                        if m == 1:
                            pool.sem_inc(s_parts, 1)
                        ins = nc.gpsimd.tensor_tensor(parts[:, t % RING, 2, m, :], rest[:, m, :],
                                                      parts[:, t % RING, 1, m, :], ALU.subtract)
                        if m == 0:
                            link(ins)
                            pool.sem_inc(s_lo, 1)
                        if t == 0 and m == 0:
                            rstd(ve1, mv1, rs1, 1, 3)
                    ins.then_inc(s_parts, 1)
                if t == 0:
                    rstd(ve1, mv1, rs1, 3, B)
                    constants()
                    pool.wait_ge(s_tbo, seen(s_tbo))
                    nc.gpsimd.tensor_tensor(x_sb[:, :, :], x_sb[:, :, :],
                                            tbo[:, :].unsqueeze(1).to_broadcast([NQ, B, D]),
                                            ALU.add).then_inc(s_xbo, 1)
                if t == B:
                    rstd(ve2, mv2, rs2, *NORMED[0], signal=s_pchain)
                    pool.wait_ge(s_pchain, seen(s_pchain))
                    pool.sem_inc(s_rstd, 1)
                    lo, hi = NORMED[0]
                    link(nc.gpsimd.tensor_tensor(mrs2[:, lo:hi], mv2[:, lo:hi, 0], rs2[:, lo:hi],
                                                 ALU.mult))
                    nc.gpsimd.tensor_scalar(nmean[:, lo:hi], mrs2[:, lo:hi], -1.0, None, ALU.mult)\
                        .then_inc(s_nmean, 1)
                if t == B + 1:
                    rstd(ve2, mv2, rs2, *NORMED[1])

            turns(pool, seen, step)
            pool.wait_ge(s_cleared, seen(s_cleared, 16))
            pool.wait_ge(s_slot, seen(s_slot))
            scatter(0, EARLY)
            rstd(ve2, mv2, rs2, *NORMED[2])
            scatter(EARLY, B - 1)
            pool.wait_ge(s_slot, seen(s_slot))
            scatter(B - 1, B)

            pool.wait_ge(s_outx, seen(s_outx, 48))
            for e in range(E):
                pool.wait_ge(s_res, seen(s_res))
                if e < E - 4:
                    pool.sem_inc(s_free, 1)
                nc.gpsimd.indirect_dma_start(
                    out_rows, bass.IndirectOffsetOnAxis(
                        ap=xin[:, e, TOKEN:TOKEN + 1].bitcast(I32), axis=0), res[:, e, :],
                    None, bounds_check=B * NQ - 1, oob_is_err=False).then_inc(s_out, 16)
            pool.wait_ge(s_out, seen(s_out, 16 * E))


def kernel(x, ctx_768, g_xattn, g_ffn, L0_xattn_Wq, L0_xattn_bq, L0_xattn_Wk, L0_xattn_bk,
           L0_xattn_Wv, L0_xattn_bv, L0_xattn_Wo, L0_xattn_bo, L0_ffn_wg, L0_ffn_W, L0_ffn_b):
    import numpy as np
    import concourse.bacc as bacc
    from concourse.bass_utils import run_bass_kernel_spmd

    def by_dim(w):
        w = np.asarray(w)
        lead = w.shape[:-1]
        return w.reshape(*lead, H // 2, 2, HD).transpose(*range(len(lead)), -2, -1, -3).reshape(*lead, D)

    def with_bias(w, b):
        laid = np.zeros((2, 128, D), w.dtype)
        laid[:, 0:KC, :] = w.reshape(2, KC, D)
        laid[1, KC, :] = b
        return laid

    arrays = {
        "x": np.asarray(x),
        "ctxT": np.asarray(ctx_768).transpose(2, 0, 1).reshape(2, KC, B, NK),
        "g_xattn": np.asarray(g_xattn), "g_ffn": np.asarray(g_ffn),
        "wq": by_dim(L0_xattn_Wq).reshape(2, 128, D), "bq": by_dim(L0_xattn_bq).reshape(1, D),
        "wk": with_bias(by_dim(L0_xattn_Wk), by_dim(L0_xattn_bk)),
        "wv": with_bias(np.asarray(L0_xattn_Wv), np.asarray(L0_xattn_bv)),
        "wo": np.asarray(L0_xattn_Wo).reshape(2, 2, 4, HD, D).transpose(2, 0, 3, 1, 4)
                .reshape(128, 2, D),
        "bo": np.asarray(L0_xattn_bo),
        "wg": np.asarray(L0_ffn_wg).reshape(2, 128, E),
        "wT": np.asarray(L0_ffn_W).transpose(0, 2, 1).reshape(E, 2, 128, D),
        "be": np.asarray(L0_ffn_b),
    }
    arrays = {f"in_{n}": np.ascontiguousarray(a) for n, a in arrays.items()}
    nc = bacc.Bacc("TRN2", target_bir_lowering=False, num_devices=1)
    args = [nc.dram_tensor(n, a.shape, mybir.dt.from_np(a.dtype), kind="ExternalInput").ap()
            for n, a in arrays.items()]
    args.append(nc.dram_tensor("out", (B, NQ, D), F32, kind="ExternalOutput").ap())
    build(nc, *args)
    return run_bass_kernel_spmd(nc, [arrays], core_ids=[0]).results[0]["out"]
```
